# Optimizing a Trainium2 kernel written in Bass

```python
import numpy as np
import jax
import jax.numpy as jnp

def _softmax(x, axis=-1):
    return jax.nn.softmax(x, axis=axis)

def _gelu(x):
    return jax.nn.gelu(x, approximate=True)

def _silu(x):
    return jax.nn.silu(x)

def _sigmoid(x):
    return jax.nn.sigmoid(x)

def _layernorm(x, axis=-1, eps=1e-05):
    m = jnp.mean(x, axis=axis, keepdims=True)
    v = jnp.var(x, axis=axis, keepdims=True)
    return (x - m) / jnp.sqrt(v + eps)

def _scatter_add(tgt, idx, src, axis=0):
    return tgt.at[idx].add(src)

def _segment_sum(src, seg, n):
    return jax.ops.segment_sum(src, seg, n)
kernel_name = 'mk_seq_postln_d1_jaxref_r4_ac0502'

def setup_inputs(seed: int=0):
    np.random.seed(seed)
    _w = jnp.asarray

    def _L0_attn_setup():
        import jax, jax.numpy as jnp
        import numpy as np
        B, L, D, H = (4, 1024, 256, 16)
        LN_EPS = 1e-05

        def _gated_delta_rule(q, k, v, lam, beta, d):

            def step(S, inp):
                k_t, v_t, q_t = inp
                S = lam * S
                u = beta * (v_t - jnp.einsum('kv,k->v', S, k_t))
                S = S + k_t[:, None] * u[None, :]
                o = jnp.einsum('kv,k->v', S, q_t)
                return (S, o)

            def scan_one(k_h, v_h, q_h):
                S0 = jnp.zeros((d, d), dtype=q.dtype)
                _, o = jax.lax.scan(step, S0, (k_h, v_h, q_h))
                return o
            return jax.vmap(scan_one)(k, v, q)
        key = jax.random.key(seed)
        k0, k1 = jax.random.split(key, 2)
        x = jax.random.normal(k0, (B, L, D), dtype=jnp.float32)
        W = jax.random.normal(k1, (D, D), dtype=jnp.float32) / jnp.sqrt(D).astype(jnp.float32)
        ln_gamma = jnp.ones((D,), dtype=jnp.float32)
        ln_beta = jnp.zeros((D,), dtype=jnp.float32)
        eta = jnp.asarray(0.01, dtype=jnp.float32)
        lam_logit = jnp.asarray(np.log(0.99) - np.log(0.01), dtype=jnp.float32)
        return {'x': x, 'W': W, 'ln_gamma': ln_gamma, 'ln_beta': ln_beta, 'eta': eta, 'lam_logit': lam_logit}
    _L0_attn_in = _L0_attn_setup()

    def _L0_ffn_setup():
        import jax, jax.numpy as jnp
        import numpy as np
        DIM = 256
        HIDDEN = 768
        SCALE = 1.0 / 127.0

        def _dequant(w_int, dtype):
            return w_int.astype(dtype) * jnp.asarray(SCALE, dtype)
        key = jax.random.key(seed)
        k_x, k_g, k_u, k_d = jax.random.split(key, 4)
        x = jax.random.normal(k_x, (4, 512, DIM), dtype=jnp.float32)
        w_gate = jax.random.randint(k_g, (HIDDEN, DIM), -127, 128, dtype=jnp.int32)
        w_up = jax.random.randint(k_u, (HIDDEN, DIM), -127, 128, dtype=jnp.int32)
        w_down = jax.random.randint(k_d, (DIM, HIDDEN), -127, 128, dtype=jnp.int32)
        return {'x': x, 'w_gate': w_gate, 'w_up': w_up, 'w_down': w_down}
    _L0_ffn_in = _L0_ffn_setup()
    _d = {'L0_attn_x': _L0_attn_in['x'], 'L0_attn_W': _L0_attn_in['W'], 'L0_attn_ln_gamma': _L0_attn_in['ln_gamma'], 'L0_attn_ln_beta': _L0_attn_in['ln_beta'], 'L0_attn_eta': _L0_attn_in['eta'], 'L0_attn_lam_logit': _L0_attn_in['lam_logit'], 'L0_ffn_w_gate': _L0_ffn_in['w_gate'], 'L0_ffn_w_up': _L0_ffn_in['w_up'], 'L0_ffn_w_down': _L0_ffn_in['w_down']}
    _x0 = _d['L0_attn_x']
    _d['L0_attn_x'] = jax.random.normal(jax.random.fold_in(jax.random.key(seed), 1), (8, 2048, 256), dtype=_x0.dtype)
    del _x0
    return _d

def reference(L0_attn_x, L0_attn_W, L0_attn_ln_gamma, L0_attn_ln_beta, L0_attn_eta, L0_attn_lam_logit, L0_ffn_w_gate, L0_ffn_w_up, L0_ffn_w_down):

    def _L0_attn_ref(x, W, ln_gamma, ln_beta, eta, lam_logit):
        import jax, jax.numpy as jnp
        import numpy as np
        B, L, D, H = (4, 1024, 256, 16)
        LN_EPS = 1e-05

        def _gated_delta_rule(q, k, v, lam, beta, d):

            def step(S, inp):
                k_t, v_t, q_t = inp
                S = lam * S
                u = beta * (v_t - jnp.einsum('kv,k->v', S, k_t))
                S = S + k_t[:, None] * u[None, :]
                o = jnp.einsum('kv,k->v', S, q_t)
                return (S, o)

            def scan_one(k_h, v_h, q_h):
                S0 = jnp.zeros((d, d), dtype=q.dtype)
                _, o = jax.lax.scan(step, S0, (k_h, v_h, q_h))
                return o
            return jax.vmap(scan_one)(k, v, q)
        Bx, Lx, Dx = x.shape
        d = Dx // H
        lam = jax.nn.sigmoid(lam_logit)
        beta = eta * (1.0 - lam) / d
        x_act = jnp.tanh(x)
        static_out = jnp.einsum('bld,ed->ble', x_act, W)

        def to_heads(t):
            return t.reshape(Bx, Lx, H, d).transpose(0, 2, 1, 3).reshape(Bx * H, Lx, d)
        q = to_heads(x_act)
        k = q
        v = to_heads(static_out)
        o = _gated_delta_rule(q, k, v, lam, beta, d)
        o_dyn = o.reshape(Bx, H, Lx, d).transpose(0, 2, 1, 3).reshape(Bx, Lx, Dx)
        y = static_out + o_dyn
        mu = jnp.mean(y, axis=-1, keepdims=True)
        var = jnp.mean(jnp.square(y - mu), axis=-1, keepdims=True)
        return (y - mu) * jax.lax.rsqrt(var + LN_EPS) * ln_gamma + ln_beta

    def _L0_ffn_ref(x, w_gate, w_up, w_down):
        import jax, jax.numpy as jnp
        import numpy as np
        DIM = 256
        HIDDEN = 768
        SCALE = 1.0 / 127.0

        def _dequant(w_int, dtype):
            return w_int.astype(dtype) * jnp.asarray(SCALE, dtype)
        wg = _dequant(w_gate, x.dtype)
        wu = _dequant(w_up, x.dtype)
        wd = _dequant(w_down, x.dtype)
        gate = jnp.einsum('bsd,hd->bsh', x, wg)
        up = jnp.einsum('bsd,hd->bsh', x, wu)
        h = jax.nn.silu(gate) * up
        return jnp.einsum('bsh,dh->bsd', h, wd)
    x = L0_attn_x
    x = _layernorm(x + _L0_attn_ref(x, L0_attn_W, L0_attn_ln_gamma, L0_attn_ln_beta, L0_attn_eta, L0_attn_lam_logit), axis=-1)
    x = _layernorm(x + _L0_ffn_ref(x, L0_ffn_w_gate, L0_ffn_w_up, L0_ffn_w_down), axis=-1)
    return x

_drawn_inputs = setup_inputs


def setup_inputs(seed=0):
    import zlib

    import numpy as np

    out = dict(_drawn_inputs(seed))
    spreads = {'L0_attn_ln_gamma': (1.0, 0.2), 'L0_attn_ln_beta': (0.0, 0.1)}
    factors = {}
    for name, (base, spread) in spreads.items():
        noise = np.random.default_rng([zlib.crc32(name.encode()), seed]).standard_normal(out[name].shape)
        drawn = base * np.exp(spread * noise) if base else spread * noise
        out[name] = jnp.asarray(drawn.astype(out[name].dtype))
    for name, factor in factors.items():
        out[name] = (out[name] * factor).astype(out[name].dtype)
    return out
```

```python
from contextlib import ExitStack

import concourse.bass as bass
from concourse import mybir

F32 = mybir.dt.float32
F16 = mybir.dt.float16
I32 = mybir.dt.int32
ALU = mybir.AluOpType
ACT = mybir.ActivationFunctionType
AX = mybir.AxisListType

P = 128
B, L, D = 8, 2048, 256
H, DH = 16, 16
C = P // B
NW = 4
T = NW * C
NS = L // T
TOK = NW * P
HID = 768
NHT = HID // P
LN_EPS = 1e-5
W_SCALE = 1.0 / 127.0
XS = 2048.0
HS = 0.25


def build(nc, x, W, ln_gamma, ln_beta, eta, lam_logit, w_gate, w_up, w_down, out):
    ctx = ExitStack()
    with ctx:
        def sb(name, shape, dt=F32):
            return ctx.enter_context(nc.sbuf_tensor(name, shape, dt))

        def sem(name):
            return ctx.enter_context(nc.semaphore(name))

        ident = sb("ident", [P, P])
        ident16 = sb("ident16", [P, P], F16)
        w_t = sb("w_t", [P, 2, D])
        wg_t = sb("wg_t", [P, 2, HID], F16)
        wu_t = sb("wu_t", [P, 2, HID], F16)
        wd_t = sb("wd_t", [P, NHT, D], F16)
        gamma = sb("gamma", [P, D])
        lnb = sb("lnb", [P, D])
        sc = sb("sc", [P, 8])
        ETA, LOGIT, OML, LAM, BETA, NBETA = range(6)
        powers = sb("powers", [P, C + 1])
        rpowers = sb("rpowers", [P, C])
        step_of = sb("step_of", [P, C])
        ctmp = sb("ctmp", [P, 2, C])
        dcol = sb("dcol", [P, 1])
        kcol = sb("kcol", [P, 1])
        nmask = sb("nmask", [P, C, C])
        mhalf = sb("mhalf", [P, NW])
        eps = sb("eps", [P, NW])
        carrier = sb("carrier", [P, 1])

        xin = sb("xin", [P, NW, D])
        xa = sb("xa", [P, NW, D])
        kt = sb("kt", [P, NW, DH, H])
        sq = sb("sq", [P, 2, D])
        nb = sb("nb", [P, 2, NW, H])
        xt = sb("xt", [P, 2, B, C, NW])
        E = [sb(f"e{p}", [P, H, B, C, NW]) for p in range(2)]
        xb = sb("xb", [P, H, C, NW])
        gs = sb("gs", [P, H, C, NW])
        gh = sb("gh", [P, C, C, NW])
        tt = sb("tt", [P, C, C, NW])
        tmp = gs[:, 0:C - 1, :, :]
        tb = sb("tb", [P, H, B, C, NW])
        kb = [sb(f"kb{w}", [P, B, DH, H]) for w in range(2)]
        v = sb("v", [P, 2, NW, D])
        S = sb("S", [P, D])
        R = sb("R", [P, 2, D])
        U = sb("U", [P, 2, D])
        y = sb("y", [P, 2, NW, D])
        xr = sb("xr", [P, NW, D])
        st1 = sb("st1", [P, NW, 6])
        mv1 = sb("mv1", [P, NW, 2])
        rs1 = sb("rs1", [P, NW])
        st2 = sb("st2", [P, NW, 6])
        mv2 = sb("mv2", [P, NW, 2])
        rs2 = sb("rs2", [P, NW])
        st3 = sb("st3", [P, NW, 6])
        mv3 = sb("mv3", [P, NW, 2])
        rs3 = sb("rs3", [P, NW])
        x1hi = sb("x1hi", [P, 2, TOK], F16)
        x1lo = sb("x1lo", [P, 2, TOK], F16)
        gate = sb("gate", [P, 2, TOK])
        hhi = sb("hhi", [P, NHT, TOK], F16)
        hlo = sb("hlo", [P, NHT, TOK], F16)

        pc = ctx.enter_context(nc.psum_tensor("pc", [P, 512], F32))
        pf = [ctx.enter_context(nc.psum_tensor(f"pf{i}", [P, 512], F32)) for i in range(2)]
        pg = [ctx.enter_context(nc.psum_tensor(f"pg{i}", [P, 512], F32)) for i in range(2)]
        pu = [ctx.enter_context(nc.psum_tensor(f"pu{i}", [P, 512], F32)) for i in range(2)]
        pd = ctx.enter_context(nc.psum_tensor("pd", [P, 512], F32))

        scr_x = nc.dram_tensor("scr_x", [2, P, B, T], F32).ap()
        scr_g = nc.dram_tensor("scr_g", [B, C, H, T], F32).ap()
        scr_t = nc.dram_tensor("scr_t", [B, H, C, T], F32).ap()

        names = dict(
            xin=64, xa=1, kt=1, sq=2, nr=2, nb=1,
            xtp=2, xt=2, vp=2, v=2,
            xtd=32, e=256, gp=2, g=2, gd=16, gh=128,
            tf=31, td=16, tb=128,
            kb0=256, kb1=256,
            kp=4, r=4, tp=4, u=4, sp=4, s=4, y1=4, y=4,
            xr=64, xrb=1, bs1=4, ba1=4, ve1=1, rs1=1, yn=4, yg=1, res=1,
            bs2=4, ba2=4, ve2=1, rs2=1, x1=4, x1p=2, x1h=2, x1l=2,
            gu=6, si=6, h=6, hh=6, hl=6, dn=2, r2=2,
            bs3=4, ba3=4, ve3=1, rs3=1, o=4, out=64)
        sems = {n: sem("s_" + n) for n in names}
        s_ld = sem("s_ld")
        s_hop = sem("s_hop")
        s_pool0 = sem("s_pool0")
        s_c = sem("s_c")
        s_a0 = sem("s_a0")
        s_ps = sem("s_ps")
        s_wt = sem("s_wt")

        def needs(eng, *events):
            values = []
            for name, q, k in events:
                k = names[name] if k is None else k
                if k <= 0:
                    q, k = q - 1, k + names[name]
                if isinstance(q, int):
                    if q >= 0:
                        values.append((name, q * names[name] + k))
                else:
                    values.append((name, eng.snap(q * names[name] + k)))
            for name, value in values:
                eng.wait_ge(sems[name], value)
                if eng.engine == mybir.EngineType.SP and (name, value) != values[-1]:
                    eng.sem_inc(s_hop, 1)

        def need(eng, name, q, k):
            needs(eng, (name, q, k))

        def done(eng, name, q):
            needs(eng, (name, q, None))

        def steps_of(eng, q):
            return [q * T + n * C if isinstance(q, int) else eng.snap(q * T + n * C) for n in range(NW)]

        def chained(eng, ins, counter, semaphore):
            counter[0] += 1
            ins.then_inc(semaphore, 1)
            eng.wait_ge(semaphore, counter[0])

        def load_x(e, eng, q, ahead=True):
            if e == "sp":
                at = steps_of(eng, q)
                done(eng, "xa", q - 1)
                for n in range(NW):
                    eng.dma_start(xin[:, n, :], x[:, bass.ds(at[n], C), :]).then_inc(sems["xin"], 16)

        def activate(e, eng, q, p):
            if e == "act":
                done(eng, "xin", q)
                done(eng, "xtp", q - 1)
                done(eng, "kt", q - 1)
                done(eng, "sq", q - 1)
                eng.activation(xa[:, :, :], xin[:, :, :], ACT.Tanh).then_inc(sems["xa"], 1)
            if e == "pool":
                done(eng, "xa", q)
                for g in range(2):
                    need(eng, "nr", q, g)
                    eng.tensor_tensor(sq[:, :, :], xa[:, 2 * g:2 * g + 2, :], xa[:, 2 * g:2 * g + 2, :],
                                      ALU.mult).then_inc(sems["sq"], 1)
            if e == "pe":
                done(eng, "xa", q)
                for half in range(2):
                    done(eng, "g", q - 1)
                    for n in range(NW):
                        last = eng.transpose(pf[half][:, n * P:(n + 1) * P], xa[:, n, half * P:(half + 1) * P],
                                             ident[:, :])
                    last.then_inc(sems["xtp"], 1)
            if e == "act":
                for half in range(2):
                    need(eng, "xtp", q, half + 1)
                    done(eng, "vp", q - 1)
                    done(eng, "xtd", q - 1)
                    eng.activation(xt[:, half, :, :, :].rearrange("p b i n -> p (b i) n"),
                                   pf[half][:, :].rearrange("p (n t) -> p t n", n=NW),
                                   ACT.Copy).then_inc(sems["xt"], 1)

        def scale_keys(e, eng, q):
            if e == "pool":
                done(eng, "xa", q)
                done(eng, "kb0", q - 1)
                done(eng, "kb1", q - 1)
                eng.tensor_tensor(kt[:, :, :, :].rearrange("p n k h -> p n h k"),
                                  xa[:, :, :].rearrange("p n (h k) -> p n h k", h=H),
                                  kcol[:, :, None, None].to_broadcast([P, NW, H, DH]), ALU.mult)\
                   .then_inc(sems["kt"], 1)

        def key_norms(e, eng, q, p):
            if e == "dve":
                done(eng, "y1", q - 2)
                for g in range(2):
                    need(eng, "sq", q, g + 1)
                    eng.tensor_reduce(nb[:, p, 2 * g:2 * g + 2, :],
                                      sq[:, :, :].rearrange("p n (h k) -> p n h k", h=H),
                                      AX.X, ALU.add).then_inc(sems["nr"], 1)
                done(eng, "nr", q)
                eng.tensor_scalar(nb[:, p, :, :], nb[:, p, :, :], sc[:, BETA:BETA + 1], -1.0,
                                  ALU.mult, ALU.add).then_inc(sems["nb"], 1)

        def spread_keys(e, eng, q, p):
            if e == "sp":
                for half in range(2):
                    needs(eng, ("xt", q, half + 1), ("e", q - 1, None))
                    eng.dma_start(scr_x[half], xt[:, half, :, :, :].rearrange("p b i n -> p b (i n)")).then_inc(sems["xtd"], 16)
                needs(eng, ("xtd", q, None), ("gp", q - 1, None), ("kp", q - 2, None))
                src = scr_x.rearrange("z (h k) b t -> k (z h) b t", k=DH)
                for b in range(B):
                    rows = slice(DH * b, DH * (b + 1))
                    eng.dma_start(E[p][rows, :, b, :, :].rearrange("k h i n -> k h (i n)"), src[:, :, b, :]).then_inc(sems["e"], 16)
                    eng.dma_start(xb[rows, :, :, :].rearrange("k h i n -> k h (i n)"), src[:, :, b, :]).then_inc(sems["e"], 16)

        def static_out(e, eng, q, p, g):
            if e == "pe":
                done(eng, "xt", q)
                for n in (2 * g, 2 * g + 1):
                    for half in range(2):
                        last = eng.matmul(pf[g][:, (n % 2) * D:(n % 2 + 1) * D],
                                          xt[:, half, :, :, n].rearrange("p b i -> p (b i)"), w_t[:, half, :],
                                          start=half == 0, stop=half == 1)
                last.then_inc(sems["vp"], 1)
            if e == "act":
                need(eng, "vp", q, g + 1)
                done(eng, "y", q - 2)
                eng.activation(v[:, p, 2 * g:2 * g + 2, :], pf[g][:, :].rearrange("p (n d) -> p n d", n=2),
                               ACT.Copy).then_inc(sems["v"], 1)

        def gram(e, eng, q, p, g):
            if e == "pe":
                done(eng, "e", q)
                need(eng, "v", q, g + 1)
                for n in (2 * g, 2 * g + 1):
                    for h in range(H):
                        c0 = (n % 2) * D + h * C
                        last = eng.matmul(pf[g][:, c0:c0 + C], E[p][:, h, :, :, n].rearrange("p b i -> p (b i)"),
                                          xb[:, h, :, n], start=True, stop=True)
                last.then_inc(sems["gp"], 1)
            if e == "act":
                need(eng, "gp", q, g + 1)
                done(eng, "tf", q - 1)
                eng.activation(gs[:, :, :, 2 * g:2 * g + 2].rearrange("p h j n -> p (h j) n"),
                               pf[g][:, :].rearrange("p (n c) -> p c n", n=2),
                               ACT.Copy).then_inc(sems["g"], 1)

        def spread_gram(e, eng, q, p):
            if e == "sp":
                needs(eng, ("g", q, None), ("gh", q - 1, None))
                eng.dma_start(scr_g.rearrange("b i h t -> (b i) (h t)"),
                              gs[:, :, :, :].rearrange("p h j n -> p (h j n)")).then_inc(sems["gd"], 16)
                needs(eng, ("gd", q, None), ("tf", q - 1, None))
                for b in range(B):
                    eng.dma_start(gh[H * b:H * (b + 1), :, :, :].rearrange("h i j n -> h i (j n)"),
                                  scr_g[b].rearrange("i h t -> h i t")).then_inc(sems["gh"], 16)

        def invert(e, eng, q, p, rows):
            if e == "dve":
                if rows[0] == 1:
                    done(eng, "gh", q)
                    done(eng, "td", q - 1)
                    eng.tensor_tensor(gh[:, :, :, :], gh[:, :, :, :],
                                      nmask[:, :, :, None].to_broadcast([P, C, C, NW]), ALU.mult)\
                       .then_inc(sems["tf"], 1)
                for i in rows:
                    need(eng, "tf", q, 2 * i - 1)
                    eng.tensor_tensor(tmp[:, 0:i, 0:i, :], tt[:, 0:i, 0:i, :],
                                      gh[:, i:i + 1, 0:i, :].to_broadcast([P, i, i, NW]), ALU.mult)\
                       .then_inc(sems["tf"], 1)
                    need(eng, "tf", q, 2 * i)
                    eng.tensor_reduce(tt[:, 0:i, i, :], tmp[:, 0:i, 0:i, :].rearrange("p m j n -> p m n j"), AX.X, ALU.add)\
                       .then_inc(sems["tf"], 1)

        def store_inverse(e, eng, q, p):
            if e == "sp":
                needs(eng, ("tf", q, None), ("tb", q - 1, None))
                eng.dma_start(scr_t.rearrange("b h j t -> (b h) (j t)"),
                              tt[:, :, :, :].rearrange("p j i n -> p (j i n)")).then_inc(sems["td"], 16)

        def load_inverse(e, eng, q, p):
            if e == "sp":
                needs(eng, ("td", q, None), ("tp", q - 1, None))
                for b in range(B):
                    eng.dma_start(tb[C * b:C * (b + 1), :, b, :, :].rearrange("j h i n -> j h (i n)"), scr_t[b].rearrange("h j t -> j h t"))\
                       .then_inc(sems["tb"], 16)

        def load_kb(e, eng, q, w):
            if e == "sp":
                needs(eng, ("kt", q, None), ("sp", q, w - 1))
                for b in range(B):
                    rows = slice(C * b, C * (b + 1))
                    eng.dma_start(kb[w % 2][rows, b, :, :], kt[rows, w, :, :]).then_inc(sems[f"kb{w % 2}"], 16)

        def chain_k(e, eng, q, p, w):
            if e == "pe":
                need(eng, "s", q, w)
                for h in range(H):
                    last = eng.matmul(pc[:, h * DH:(h + 1) * DH], E[p][:, h, :, :, w].rearrange("p b i -> p (b i)"),
                                      S[:, h * DH:(h + 1) * DH], start=True, stop=True)
                last.then_inc(sems["kp"], 1)
            if e == "dve":
                need(eng, "kp", q, w + 1)
                need(eng, "v", q, w // 2 + 1)
                eng.scalar_tensor_tensor(R[:, w % 2, :], pc[:, 0:D], dcol[:, 0:1], v[:, p, w, :],
                                         ALU.mult, ALU.add).then_inc(sems["r"], 1)

        def chain_t(e, eng, q, p, w):
            if e == "pe":
                need(eng, "r", q, w + 1)
                done(eng, "tb", q)
                for h in range(H):
                    last = eng.matmul(pc[:, h * DH:(h + 1) * DH], tb[:, h, :, :, w].rearrange("p b i -> p (b i)"),
                                      R[:, w % 2, h * DH:(h + 1) * DH], start=True, stop=True)
                last.then_inc(sems["tp"], 1)
            if e == "dve":
                need(eng, "tp", q, w + 1)
                need(eng, "y1", q, w - 1)
                eng.tensor_copy(U[:, w % 2, :], pc[:, 0:D]).then_inc(sems["u"], 1)

        def chain_s(e, eng, q, p, w):
            if e == "pe":
                need(eng, "u", q, w + 1)
                need(eng, f"kb{w % 2}", q, 128 * (w // 2 + 1))
                for h in range(H):
                    last = eng.matmul(pc[:, h * DH:(h + 1) * DH], kb[w % 2][:, :, :, h].rearrange("p b k -> p (b k)"),
                                      U[:, w % 2, h * DH:(h + 1) * DH], start=True, stop=True)
                last.then_inc(sems["sp"], 1)
            if e == "dve":
                need(eng, "sp", q, w + 1)
                eng.scalar_tensor_tensor(S[:, :], S[:, :], powers[:, C:C + 1], pc[:, 0:D],
                                         ALU.mult, ALU.add).then_inc(sems["s"], 1)

        def attention_out(e, eng, q, p, w):
            if e == "pool":
                need(eng, "u", q, w + 1)
                done(eng, "nb", q)
                done(eng, "yg", q - 2)
                eng.tensor_tensor(y[:, p, w, :].rearrange("p (h d) -> p h d", h=H),
                                  U[:, w % 2, :].rearrange("p (h d) -> p h d", h=H),
                                  nb[:, p, w, :, None].to_broadcast([P, H, DH]), ALU.mult)\
                   .then_inc(sems["y1"], 1)
            if e == "dve":
                need(eng, "y1", q, w + 1)
                eng.scalar_tensor_tensor(y[:, p, w, :], v[:, p, w, :], 2.0, y[:, p, w, :],
                                         ALU.mult, ALU.add).then_inc(sems["y"], 1)

        def load_residual(e, eng, q):
            if e == "sp":
                at = steps_of(eng, q)
                done(eng, "out", q - 1)
                for n in range(NW):
                    eng.dma_start(xr[:, n, :], x[:, bass.ds(at[n], C), :]).then_inc(sems["xr"], 16)
            if e == "pool":
                done(eng, "xr", q)
                eng.tensor_tensor(xr[:, :, :], xr[:, :, :], lnb[:, None, :].to_broadcast([P, NW, D]), ALU.add)\
                   .then_inc(sems["xrb"], 1)

        def statistics(e, eng, q, z, src, ready, st, mv, rs, prev):
            if e == "dve":
                for n in range(NW):
                    ready(n)
                    eng.bn_stats(st[:, n, :], src[:, n, :]).then_inc(sems[f"bs{z}"], 1)
                done(eng, prev, q - 1)
                for n in range(NW):
                    if n == 0:
                        done(eng, f"bs{z}", q)
                        eng.memset(carrier[:, :], 0.0)
                    eng.bn_aggr(mv[:, n, :], st[:, n, :]).then_inc(sems[f"ba{z}"], 1)
            if e == "pool":
                done(eng, f"ba{z}", q)
                done(eng, prev, q - 1)
                eng.tensor_tensor(rs[:, :], mv[:, :, 1], eps[:, :], ALU.add).then_inc(sems[f"ve{z}"], 1)
                done(eng, f"ve{z}", q)
                eng.tensor_tensor(rs[:, :], rs[:, :], mhalf[:, :], ALU.pow).then_inc(sems[f"rs{z}"], 1)

        def normalise(e, eng, q, z, dst, src, mv, rs, name):
            if e == "dve":
                done(eng, f"rs{z}", q)
                for n in range(NW):
                    eng.tensor_scalar(dst[:, n, :], src[:, n, :], mv[:, n, 0:1], rs[:, n:n + 1],
                                      ALU.subtract, ALU.mult).then_inc(sems[name], 1)

        def attention_norm(e, eng, q, p):
            statistics(e, eng, q, 1, y[:, p], lambda n: done(eng, "y", q), st1, mv1, rs1, "yn")
            normalise(e, eng, q, 1, y[:, p], y[:, p], mv1, rs1, "yn")
            if e == "pool":
                done(eng, "yn", q)
                eng.tensor_tensor(y[:, p], y[:, p], gamma[:, None, :].to_broadcast([P, NW, D]), ALU.mult)\
                   .then_inc(sems["yg"], 1)
            if e == "dve":
                done(eng, "yg", q)
                done(eng, "xrb", q)
                eng.tensor_tensor(xr[:, :, :], xr[:, :, :], y[:, p], ALU.add).then_inc(sems["res"], 1)

        def first_norm(e, eng, q):
            statistics(e, eng, q, 2, xr, lambda n: done(eng, "res", q), st2, mv2, rs2, "x1")
            normalise(e, eng, q, 2, xr, xr, mv2, rs2, "x1")

        def transpose_x1(e, eng, q):
            if e == "pe":
                done(eng, "x1", q)
                for half in range(2):
                    done(eng, "si", q - 1)
                    for n in range(NW):
                        last = eng.transpose(pg[half][:, n * P:(n + 1) * P], xr[:, n, half * P:(half + 1) * P],
                                             ident[:, :])
                    last.then_inc(sems["x1p"], 1)
            for half in range(2):
                if e == "act":
                    need(eng, "x1p", q, half + 1)
                    done(eng, "gu", q - 1)
                    eng.activation(x1hi[:, half, :], pg[half][:, :], ACT.Copy, scale=XS).then_inc(sems["x1h"], 1)
                if e == "dve":
                    need(eng, "x1h", q, half + 1)
                    eng.scalar_tensor_tensor(x1lo[:, half, :], pg[half][:, :], XS, x1hi[:, half, :],
                                             ALU.mult, ALU.subtract).then_inc(sems["x1l"], 1)

        def hidden(e, eng, q, t):
            k = t % 2
            if e == "pe":
                done(eng, "x1l", q)
                if t >= 2:
                    need(eng, "h", q, t - 1)
                for bank, wt in ((pg[k], wg_t), (pu[k], wu_t)):
                    for half in range(2):
                        for part, xp in enumerate((x1hi, x1lo)):
                            last = eng.matmul(bank[:, :], wt[:, half, t * P:(t + 1) * P], xp[:, half, :],
                                              start=half + part == 0, stop=half + part == 2)
                last.then_inc(sems["gu"], 1)
            if e == "act":
                need(eng, "gu", q, t + 1)
                need(eng, "hl", q, t - 1)
                eng.activation(gate[:, k, :], pg[k][:, :], ACT.Silu, scale=W_SCALE / XS).then_inc(sems["si"], 1)
            if e == "dve":
                need(eng, "si", q, t + 1)
                eng.scalar_tensor_tensor(gate[:, k, :], pu[k][:, :], W_SCALE * HS / XS, gate[:, k, :],
                                         ALU.mult, ALU.mult).then_inc(sems["h"], 1)
            if e == "act":
                need(eng, "h", q, t + 1)
                done(eng, "dn", q - 1)
                eng.activation(hhi[:, t, :], gate[:, k, :], ACT.Copy).then_inc(sems["hh"], 1)
            if e == "dve":
                need(eng, "hh", q, t + 1)
                eng.tensor_tensor(hlo[:, t, :], gate[:, k, :], hhi[:, t, :], ALU.subtract).then_inc(sems["hl"], 1)

        def down(e, eng, q, g):
            if e == "pe":
                done(eng, "hl", q)
                need(eng, "r2", q, g)
                for n in (2 * g, 2 * g + 1):
                    for t in range(NHT):
                        for part, hp in enumerate((hhi, hlo)):
                            last = eng.matmul(pd[:, (n % 2) * D:(n % 2 + 1) * D], hp[:, t, n * P:(n + 1) * P],
                                              wd_t[:, t, :], start=t + part == 0, stop=t + part == NHT)
                last.then_inc(sems["dn"], 1)
            if e == "dve":
                need(eng, "dn", q, g + 1)
                eng.scalar_tensor_tensor(xr[:, 2 * g:2 * g + 2, :], pd[:, :].rearrange("p (n d) -> p n d", n=2),
                                         W_SCALE / HS, xr[:, 2 * g:2 * g + 2, :], ALU.mult, ALU.add)\
                   .then_inc(sems["r2"], 1)

        def last_norm(e, eng, q):
            statistics(e, eng, q, 3, xr, lambda n: need(eng, "r2", q, n // 2 + 1), st3, mv3, rs3, "o")
            normalise(e, eng, q, 3, xr, xr, mv3, rs3, "o")

        def store_out(e, eng, q):
            if e == "sp":
                at = steps_of(eng, q)
                for n in range(NW):
                    need(eng, "o", q, n + 1)
                    eng.dma_start(out[:, bass.ds(at[n], C), :], xr[:, n, :]).then_inc(sems["out"], 16)

        def step(e, eng, s, p, chain=True, front=True, post=True):
            f, o_ = s + 1, s - 1
            fp, op = 1 - p, 1 - p

            def at(w, c):
                if chain:
                    (chain_k, chain_t, chain_s)[c](e, eng, s, p, w)
                    if c == 2:
                        attention_out(e, eng, s, p, w)

            if chain:
                load_kb(e, eng, s, 0)
                load_inverse(e, eng, s, p)
                load_kb(e, eng, s, 1)
            at(0, 0)
            if front:
                activate(e, eng, f, fp)
                if not (isinstance(s, int) and s >= NS - 2):
                    load_x(e, eng, f + 1)
                spread_keys(e, eng, f, fp)
                key_norms(e, eng, f, fp)
            if post:
                load_residual(e, eng, o_)
            at(0, 1)
            if front:
                static_out(e, eng, f, fp, 0)
            if post:
                attention_norm(e, eng, o_, op)
            at(0, 2)
            if front:
                static_out(e, eng, f, fp, 1)
            if post:
                first_norm(e, eng, o_)
            if chain:
                load_kb(e, eng, s, 2)
            at(1, 0)
            if front:
                gram(e, eng, f, fp, 0)
            at(1, 1)
            if front:
                gram(e, eng, f, fp, 1)
                spread_gram(e, eng, f, fp)
            at(1, 2)
            if post:
                transpose_x1(e, eng, o_)
            if chain:
                load_kb(e, eng, s, 3)
            at(2, 0)
            if post:
                hidden(e, eng, o_, 0)
            if front:
                invert(e, eng, f, fp, range(1, 7))
            at(2, 1)
            if post:
                hidden(e, eng, o_, 1)
            if front:
                invert(e, eng, f, fp, range(7, 10))
            if front:
                scale_keys(e, eng, f)
            at(2, 2)
            if post:
                hidden(e, eng, o_, 2)
            if front:
                invert(e, eng, f, fp, range(10, 12))
            at(3, 0)
            if post:
                hidden(e, eng, o_, 3)
            if front:
                invert(e, eng, f, fp, range(12, 14))
            at(3, 1)
            if post:
                hidden(e, eng, o_, 4)
            if front:
                invert(e, eng, f, fp, range(14, 16))
                store_inverse(e, eng, f, fp)
            at(3, 2)
            if post:
                hidden(e, eng, o_, 5)
                down(e, eng, o_, 0)
                down(e, eng, o_, 1)
                last_norm(e, eng, o_)
                store_out(e, eng, o_)

        def program(e, eng):
            load_x(e, eng, 0)
            step(e, eng, -1, 1, chain=False, post=False)
            step(e, eng, 0, 0, post=False)
            step(e, eng, 1, 1)
            with eng.Fori(1, NS // 2 - 1) as i:
                step(e, eng, i * 2, 0)
                step(e, eng, i * 2 + 1, 1)
            step(e, eng, NS - 2, 0)
            step(e, eng, NS - 1, 1, front=False)
            step(e, eng, NS, 0, chain=False, front=False)
            if e == "sp":
                done(eng, "out", NS - 1)

        block = ctx.enter_context(nc.Block())
        w_nat = v[:, 0, 0:2, :]
        wg_nat = E[1][:, 0:4].rearrange("p h b i n -> p (h b i n)")[:, 0:NHT * D].bitcast(I32)\
            .rearrange("p (t d) -> p t d", t=NHT)
        wu_nat = E[1][:, 4:8].rearrange("p h b i n -> p (h b i n)")[:, 0:NHT * D].bitcast(I32)\
            .rearrange("p (t d) -> p t d", t=NHT)
        wd_nat = E[1][:, 8:12].rearrange("p h b i n -> p (h b i n)")[:, 0:2 * HID].bitcast(I32)\
            .rearrange("p (t d) -> p t d", t=2)
        wg16 = tb[:, 0:2].rearrange("p h b i n -> p (h b i n)").bitcast(F16)[:, 0:NHT * D]\
            .rearrange("p (t d) -> p t d", t=NHT)
        wu16 = tb[:, 2:4].rearrange("p h b i n -> p (h b i n)").bitcast(F16)[:, 0:NHT * D]\
            .rearrange("p (t d) -> p t d", t=NHT)
        wd16 = tb[:, 4:6].rearrange("p h b i n -> p (h b i n)").bitcast(F16)[:, 0:2 * HID]\
            .rearrange("p (t d) -> p t d", t=2)
        ps16 = [pg[0][:, 0:256].bitcast(F16), pg[1][:, 0:256].bitcast(F16)]

        jobs = []
        for dst, src in ((wg_t, wg16), (wu_t, wu16)):
            for half in range(2):
                for t0 in range(0, NHT, 2):
                    jobs.append(([src[:, t0 + a, half * P:(half + 1) * P] for a in range(2)],
                                 dst[:, half, t0 * P:(t0 + 2) * P]))
        for t in range(NHT):
            jobs.append(([wd16[:, a, t * P:(t + 1) * P] for a in range(2)], wd_t[:, t, :]))
        NJ = len(jobs)
        N_SETUP = 4 + 5 + 2 * C + 7 + 1 + (C - 1) + 1 + C

        @block.sync
        def _(eng):
            bc = lambda a, n: a.rearrange("(o n) -> o n", o=1).to_broadcast([P, n])
            eng.dma_start(sc[:, ETA:ETA + 1], eta.to_broadcast([P, 1])).then_inc(s_ld, 16)
            eng.dma_start(sc[:, LOGIT:LOGIT + 1], lam_logit.to_broadcast([P, 1])).then_inc(s_ld, 16)
            eng.dma_start(w_nat, W.rearrange("(a p) d -> p a d", p=P)).then_inc(s_ld, 16)
            eng.dma_start(wg_nat, w_gate.rearrange("(t p) d -> p t d", p=P)).then_inc(s_ld, 16)
            eng.dma_start(wu_nat, w_up.rearrange("(t p) d -> p t d", p=P)).then_inc(s_ld, 16)
            eng.dma_start(wd_nat, w_down.rearrange("(t p) d -> p t d", p=P)).then_inc(s_ld, 16)
            eng.dma_start(gamma[:, :], bc(ln_gamma, D)).then_inc(s_ld, 16)
            eng.dma_start(lnb[:, :], bc(ln_beta, D)).then_inc(s_ld, 16)
            eng.wait_ge(s_wt, NJ + 1)
            eng.wait_ge(s_pool0, 10)
            program("sp", eng)

        @block.gpsimd
        def _(eng):
            n = [0]
            chained(eng, eng.memset(ident[:, :], 0.0), n, s_pool0)
            chained(eng, eng.affine_select(out=ident[:, :], in_=ident[:, :], compare_op=ALU.not_equal, fill=1.0,
                                           base=0, pattern=[[-1, P]], channel_multiplier=1), n, s_pool0)
            chained(eng, eng.memset(mhalf[:, :], -0.5), n, s_pool0)
            chained(eng, eng.memset(eps[:, :], LN_EPS), n, s_pool0)
            chained(eng, eng.memset(E[0][:, :, :, :, :], 0.0), n, s_pool0)
            chained(eng, eng.memset(kb[0][:, :, :, :], 0.0), n, s_pool0)
            chained(eng, eng.memset(kb[1][:, :, :, :], 0.0), n, s_pool0)
            chained(eng, eng.memset(S[:, :], 0.0), n, s_pool0)
            eng.wait_ge(s_wt, NJ + 1)
            chained(eng, eng.memset(E[1][:, :, :, :, :], 0.0), n, s_pool0)
            chained(eng, eng.memset(tb[:, :, :, :, :], 0.0), n, s_pool0)
            eng.wait_ge(s_c, N_SETUP)
            program("pool", eng)

        @block.scalar
        def _(eng):
            eng.wait_ge(s_ld, 16 * 8)
            eng.activation(sc[:, OML:OML + 1], sc[:, LOGIT:LOGIT + 1], ACT.Sigmoid, scale=-1.0).then_inc(s_a0, 1)
            program("act", eng)

        @block.vector
        def _(eng):
            n = [0]

            def link(ins):
                chained(eng, ins, n, s_c)

            eng.wait_ge(s_pool0, 2)
            link(eng.tensor_copy(ident16[:, :], ident[:, :]))
            eng.wait_ge(s_ld, 16 * 8)
            link(eng.tensor_copy(wg16, wg_nat))
            link(eng.tensor_copy(wu16, wu_nat))
            link(eng.tensor_copy(wd16, wd_nat))
            n_w = n[0]
            for j, (_, dst) in enumerate(jobs):
                eng.wait_ge(s_ps, j + 1)
                eng.tensor_copy(dst, ps16[j % 2][:, 0:2 * P]).then_inc(s_wt, 1)
            eng.wait_ge(s_ps, NJ + 1)
            eng.tensor_copy(w_t[:, :, :], pu[0][:, :].rearrange("p (a d) -> p a d", a=2)).then_inc(s_wt, 1)
            eng.wait_ge(s_a0, 1)
            link(eng.tensor_scalar(sc[:, LAM:LAM + 1], sc[:, OML:OML + 1], -1.0, 1.0, ALU.mult, ALU.add))
            link(eng.tensor_tensor(sc[:, BETA:BETA + 1], sc[:, ETA:ETA + 1], sc[:, OML:OML + 1], ALU.mult))
            link(eng.tensor_scalar(sc[:, BETA:BETA + 1], sc[:, BETA:BETA + 1], 1.0 / DH, None, ALU.mult))
            link(eng.tensor_scalar(sc[:, NBETA:NBETA + 1], sc[:, BETA:BETA + 1], -1.0, None, ALU.mult))
            link(eng.memset(powers[:, 0:1], 1.0))
            for m in range(C):
                link(eng.tensor_scalar(powers[:, m + 1:m + 2], powers[:, m:m + 1], sc[:, LAM:LAM + 1], None,
                                       ALU.mult))
            for m in range(C):
                link(eng.tensor_copy(rpowers[:, m:m + 1], powers[:, C - 1 - m:C - m]))
            link(eng.tensor_reduce(step_of[:, :], ident[:, :].rearrange("p (b i) -> p i b", b=B), AX.X, ALU.add))
            link(eng.tensor_tensor(ctmp[:, 0, :], step_of[:, :], powers[:, 1:C + 1], ALU.mult))
            link(eng.tensor_tensor(ctmp[:, 1, :], step_of[:, :], rpowers[:, :], ALU.mult))
            link(eng.tensor_reduce(dcol[:, :], ctmp[:, 0, :], AX.X, ALU.add))
            link(eng.tensor_scalar(dcol[:, :], dcol[:, :], -1.0, None, ALU.mult))
            link(eng.tensor_reduce(kcol[:, :], ctmp[:, 1, :], AX.X, ALU.add))
            link(eng.tensor_scalar(kcol[:, :], kcol[:, :], sc[:, BETA:BETA + 1], None, ALU.mult))
            link(eng.memset(nmask[:, :, :], 0.0))
            flat = nmask[:, :, :].rearrange("p i j -> p (i j)")
            for d in range(1, C):
                link(eng.tensor_scalar(flat[:, C * d:C * C:C + 1],
                                       powers[:, d:d + 1].to_broadcast([P, C - d]),
                                       sc[:, NBETA:NBETA + 1], None, ALU.mult))
            link(eng.memset(tt[:, :, :, :], 0.0))
            for j in range(C):
                link(eng.memset(tt[:, j, j, :], 1.0))
            assert n[0] == N_SETUP
            program("dve", eng)

        @block.tensor
        def _(eng):
            eng.wait_ge(s_pool0, 2)
            eng.wait_ge(s_c, 4)
            for j, (srcs, _) in enumerate(jobs):
                if j >= 2:
                    eng.wait_ge(s_wt, j - 1)
                for a, src in enumerate(srcs):
                    last = eng.transpose(ps16[j % 2][:, a * P:(a + 1) * P], src, ident16[:, :])
                last.then_inc(s_ps, 1)
            for half in range(2):
                for a in range(2):
                    last = eng.transpose(pu[0][:, half * D + a * P:half * D + (a + 1) * P],
                                         w_nat[:, a, half * P:(half + 1) * P], ident[:, :])
            last.then_inc(s_ps, 1)
            eng.wait_ge(s_wt, NJ + 1)
            program("pe", eng)


_INS = ['L0_attn_x', 'L0_attn_W', 'L0_attn_ln_gamma', 'L0_attn_ln_beta', 'L0_attn_eta', 'L0_attn_lam_logit',
        'L0_ffn_w_gate', 'L0_ffn_w_up', 'L0_ffn_w_down']


def kernel(**inputs):
    import numpy as _np
    import concourse.bacc as _bacc
    from concourse.bass_utils import run_bass_kernel_spmd as _run

    nc = _bacc.Bacc("TRN2", target_bir_lowering=False, num_devices=1)
    arrays, args = {}, []
    for name in _INS:
        a = _np.ascontiguousarray(inputs[name])
        if a.ndim == 0:
            a = a.reshape(1)
        arrays[name] = a
        args.append(nc.dram_tensor(name, a.shape, mybir.dt.from_np(a.dtype), kind="ExternalInput").ap())
    args.append(nc.dram_tensor("y_out", (B, L, D), F32, kind="ExternalOutput").ap())
    build(nc, *args)
    r = _run(nc, [arrays], core_ids=[0])
    return r.results[0]["y_out"]
```

```python
from contextlib import ExitStack

import concourse.bass as bass
from concourse import mybir

F32 = mybir.dt.float32
F16 = mybir.dt.float16
I32 = mybir.dt.int32
ALU = mybir.AluOpType
ACT = mybir.ActivationFunctionType
AX = mybir.AxisListType

P = 128
B, L, D = 8, 2048, 256
H, DH = 16, 16
C = P // B
NW = 4
T = NW * C
NS = L // T
TOK = NW * P
HID = 768
NHT = HID // P
LN_EPS = 1e-5
W_SCALE = 1.0 / 127.0
XS = 2048.0
WS = 1024.0
KS = 4096.0
TS = 256.0
RS = 64.0
SS = 1024.0
HS = 0.25


def build(nc, x, W, ln_gamma, ln_beta, eta, lam_logit, w_gate, w_up, w_down, out):
    ctx = ExitStack()
    with ctx:
        def sb(name, shape, dt=F32):
            return ctx.enter_context(nc.sbuf_tensor(name, shape, dt))

        def sem(name):
            return ctx.enter_context(nc.semaphore(name))

        ident = sb("ident", [P, P])
        ident16 = sb("ident16", [P, P], F16)
        w_t = sb("w_t", [P, 2, 2, D], F16)
        wg_t = sb("wg_t", [P, 2, HID], F16)
        wu_t = sb("wu_t", [P, 2, HID], F16)
        wd_t = sb("wd_t", [P, NHT, D], F16)
        gamma = sb("gamma", [P, D])
        lnb = sb("lnb", [P, D])
        sc = sb("sc", [P, 8])
        ETA, LOGIT, OML, LAM, BETA, NBETA, BETAS, BETAR = range(8)
        powers = sb("powers", [P, C + 1])
        rpowers = sb("rpowers", [P, C])
        step_of = sb("step_of", [P, C])
        ctmp = sb("ctmp", [P, 2, C])
        dcol = sb("dcol", [P, 1])
        kcol = sb("kcol", [P, 1])
        nmask = sb("nmask", [P, C, C])
        mhalf = sb("mhalf", [P, NW])
        eps = sb("eps", [P, NW])
        carrier = sb("carrier", [P, 1])

        xa = sb("xa", [P, NW, D])
        k16 = sb("k16", [P, 2, DH, 2, H, 2], F16)
        nb = sb("nb", [P, 2, NW, H])
        xt_x1 = sb("xt_x1", [P, 2 * 2 * TOK], F16)
        xt = xt_x1[:, :].rearrange("p (g b i z n) -> p g b i z n", g=2, b=B, i=C, z=2)
        x1hi = xt_x1[:, 0:2 * TOK].rearrange("p (g t) -> p g t", g=2)
        x1lo = xt_x1[:, 2 * TOK:].rearrange("p (g t) -> p g t", g=2)
        E = [sb(f"e{p}", [P, H, B, C, 2, NW], F16) for p in range(2)]
        gs = sb("gs", [P, H, C, NW])
        gh = sb("gh", [P, C, C, NW])
        xb = gh[:, :, :, :].rearrange("p i j n -> p (i j n)").bitcast(F16)\
            .rearrange("p (h i z n) -> p h i z n", h=H, i=C, z=2)
        tt = sb("tt", [P, C, C, NW])
        tmp = gs[:, 0:C - 1, :, :]
        t16 = gs[:, :, :, :].rearrange("p h j n -> p (h j n)").bitcast(F16)\
            .rearrange("p (j i z n) -> p j i z n", j=C, i=C, z=2)
        tb = sb("tb", [P, H, B, C, 2, NW], F16)
        kb = [sb(f"kb{g}", [P, B, DH, 2, H, 2], F16) for g in range(2)]
        v = sb("v", [P, 2, NW, D])
        S = sb("S", [P, D])
        Sl = sb("Sl", [P, D])
        S16 = sb("S16", [P, 2, D], F16)
        R = sb("R", [P, D])
        R16 = sb("R16", [P, 2, D], F16)
        U16 = sb("U16", [P, 2, 2, D], F16)
        y = sb("y", [P, NW, D])
        xr = sb("xr", [P, NW, D])
        st1 = sb("st1", [P, NW, 6])
        mv1 = sb("mv1", [P, NW, 2])
        rs1 = sb("rs1", [P, NW])
        st2 = sb("st2", [P, NW, 6])
        mv2 = sb("mv2", [P, NW, 2])
        rs2 = sb("rs2", [P, NW])
        st3 = sb("st3", [P, NW, 6])
        mv3 = sb("mv3", [P, NW, 2])
        rs3 = sb("rs3", [P, NW])
        gate = sb("gate", [P, 2, TOK])
        sq = gate[:, 0, :].rearrange("p (n d) -> p n d", n=2)
        hhi = sb("hhi", [P, NHT, TOK], F16)
        hlo = sb("hlo", [P, NHT, TOK], F16)

        pc = ctx.enter_context(nc.psum_tensor("pc", [P, 512], F32))
        pf = [ctx.enter_context(nc.psum_tensor(f"pf{i}", [P, 512], F32)) for i in range(2)]
        pg = [ctx.enter_context(nc.psum_tensor(f"pg{i}", [P, 512], F32)) for i in range(2)]
        pu = [ctx.enter_context(nc.psum_tensor(f"pu{i}", [P, 512], F32)) for i in range(2)]
        pd = ctx.enter_context(nc.psum_tensor("pd", [P, 512], F32))

        scr_x = nc.dram_tensor("scr_x", [2, P, B, 2 * T], F16).ap()
        scr_g = nc.dram_tensor("scr_g", [B, C, H, T], F32).ap()
        scr_t = nc.dram_tensor("scr_t", [B, H, C, 2 * T], F16).ap()

        names = dict(
            xin=64, xa=1, k16h=4, k16=4, sq=2, nr=2, nb=1,
            xtp=2, xth=2, xt=2, vp=2, v=2,
            xtd=32, e=256, gp=2, g=2, gd=16, gh=128,
            tf=31, t16h=1, t16=1, td=16, tb=128,
            kb0=128, kb1=128,
            kp=4, r0=4, rh=4, r=4, tp=4, uh=4, u=4, sp=4, s0=4, sh=4, s=4, sl=4, y0=4, y1=4, y=4,
            xr=64, xrb=1, bs1=4, ba1=4, ve1=1, rs1=1, yn=4, yg=1, res=1,
            bs2=4, ba2=4, ve2=1, rs2=1, x1=4, x1p=2, x1h=2, x1l=2,
            gu=6, si=6, h=6, hh=6, hl=6, dn=2, r2=2,
            bs3=4, ba3=4, ve3=1, rs3=1, o=4, out=64)
        sems = {n: sem("s_" + n) for n in names}
        s_ld = sem("s_ld")
        s_hop = sem("s_hop")
        s_pool0 = sem("s_pool0")
        s_c = sem("s_c")
        s_a0 = sem("s_a0")
        s_ps = sem("s_ps")
        s_wt = sem("s_wt")

        def needs(eng, *events):
            values = []
            for name, q, k in events:
                k = names[name] if k is None else k
                if k <= 0:
                    q, k = q - 1, k + names[name]
                if isinstance(q, int):
                    if q >= 0:
                        values.append((name, q * names[name] + k))
                else:
                    values.append((name, eng.snap(q * names[name] + k)))
            for name, value in values:
                eng.wait_ge(sems[name], value)
                if eng.engine == mybir.EngineType.SP and (name, value) != values[-1]:
                    eng.sem_inc(s_hop, 1)

        def need(eng, name, q, k):
            needs(eng, (name, q, k))

        def done(eng, name, q):
            needs(eng, (name, q, None))

        def is_last(q):
            return isinstance(q, int) and q + 2 >= NS

        def steps_of(eng, q):
            return [q * T + n * C if isinstance(q, int) else eng.snap(q * T + n * C) for n in range(NW)]

        def chained(eng, ins, counter, semaphore):
            counter[0] += 1
            ins.then_inc(semaphore, 1)
            eng.wait_ge(semaphore, counter[0])

        PARTS = [(0, 0), (0, 1), (1, 0), (1, 1)]
        PARTS3 = [(half, a, b) for half in range(2) for a, b in PARTS]

        def load_x(e, eng, q, ahead=True):
            if e == "sp":
                at = steps_of(eng, q)
                needs(eng, ("xtp", q - 1, None), ("sq", q - 1, None), ("k16", q - 1, None))
                for n in range(NW):
                    eng.dma_start(xa[:, n, :], x[:, bass.ds(at[n], C), :]).then_inc(sems["xin"], 16)

        def activate(e, eng, q, p):
            if e == "act":
                done(eng, "xin", q)
                eng.activation(xa[:, :, :], xa[:, :, :], ACT.Tanh).then_inc(sems["xa"], 1)
            if e == "pool":
                done(eng, "xa", q)
                need(eng, "hl", q - 3, NHT - 1)
                for g in range(2):
                    need(eng, "nr", q, g)
                    eng.tensor_tensor(sq[:, :, :], xa[:, 2 * g:2 * g + 2, :], xa[:, 2 * g:2 * g + 2, :],
                                      ALU.mult).then_inc(sems["sq"], 1)
            if e == "pe":
                done(eng, "xa", q)
                done(eng, "g", q - 1)
                for half in range(2):
                    for n in range(NW):
                        last = eng.transpose(pf[half][:, n * P:(n + 1) * P], xa[:, n, half * P:(half + 1) * P],
                                             ident[:, :])
                    last.then_inc(sems["xtp"], 1)
            for half in range(2):
                src = pf[half][:, :].rearrange("p (n t) -> p t n", n=NW)
                dst = xt[:, half].rearrange("p b i z n -> p (b i) z n")
                if e == "act":
                    need(eng, "xtp", q, half + 1)
                    done(eng, "gu", q - 3)
                    eng.activation(dst[:, :, 0, :], src, ACT.Copy, scale=KS).then_inc(sems["xth"], 1)
                if e == "dve":
                    need(eng, "xth", q, half + 1)
                    eng.scalar_tensor_tensor(dst[:, :, 1, :], src, KS, dst[:, :, 0, :], ALU.mult, ALU.subtract)\
                       .then_inc(sems["xt"], 1)

        def scale_keys(e, eng, q):
            for g in range(2):
                src = xa[:, 2 * g:2 * g + 2, :].rearrange("p m (h k) -> p m k h", h=H)
                dst = k16[:, g].rearrange("p k z h m -> p z m k h")
                for m in range(2):
                    if e == "act":
                        if m == 0 and g == 0:
                            done(eng, "kb0", q - 1)
                            done(eng, "kb1", q - 1)
                        eng.activation(dst[:, 0, m], src[:, m], ACT.Copy, scale=kcol[:, 0:1])\
                           .then_inc(sems["k16h"], 1)
                    if e == "dve":
                        need(eng, "k16h", q, 2 * g + m + 1)
                        eng.scalar_tensor_tensor(dst[:, 1, m], src[:, m], kcol[:, 0:1], dst[:, 0, m],
                                                 ALU.mult, ALU.subtract).then_inc(sems["k16"], 1)

        def key_norms(e, eng, q, p):
            if e == "dve":
                done(eng, "y1", q - 2)
                for g in range(2):
                    need(eng, "sq", q, g + 1)
                    eng.tensor_reduce(nb[:, p, 2 * g:2 * g + 2, :],
                                      sq[:, :, :].rearrange("p n (h k) -> p n h k", h=H),
                                      AX.X, ALU.add).then_inc(sems["nr"], 1)
                done(eng, "nr", q)
                eng.tensor_scalar(nb[:, p, :, :], nb[:, p, :, :], sc[:, BETAR:BETAR + 1], -1.0 / RS,
                                  ALU.mult, ALU.add).then_inc(sems["nb"], 1)

        def spread_keys(e, eng, q, p):
            if e == "sp":
                for half in range(2):
                    needs(eng, ("xt", q, half + 1), ("e", q - 1, None))
                    eng.dma_start(scr_x[half], xt[:, half].rearrange("p b i z n -> p b (i z n)")).then_inc(sems["xtd"], 16)
                needs(eng, ("xtd", q, None), ("tf", q - 1, None), ("kp", q - 2, None))
                src = scr_x.rearrange("z (h k) b t -> k (z h) b t", k=DH)
                for b in range(B):
                    rows = slice(DH * b, DH * (b + 1))
                    eng.dma_start(E[p][rows, :, b].rearrange("k h i z n -> k h (i z n)"), src[:, :, b, :]).then_inc(sems["e"], 16)
                    eng.dma_start(xb[rows].rearrange("k h i z n -> k h (i z n)"), src[:, :, b, :]).then_inc(sems["e"], 16)

        def static_out(e, eng, q, p, g):
            if e == "pe":
                done(eng, "xt", q)
                for n in (2 * g, 2 * g + 1):
                    for half, xz, wz in PARTS3:
                        last = eng.matmul(pf[g][:, (n % 2) * D:(n % 2 + 1) * D],
                                          xt[:, half, :, :, xz, n].rearrange("p b i -> p (b i)"),
                                          w_t[:, half, wz, :], start=(half, xz, wz) == PARTS3[0],
                                          stop=(half, xz, wz) == PARTS3[-1])
                last.then_inc(sems["vp"], 1)
            if e == "act":
                need(eng, "vp", q, g + 1)
                done(eng, "y", q - 2)
                eng.activation(v[:, p, 2 * g:2 * g + 2, :], pf[g][:, :].rearrange("p (n d) -> p n d", n=2),
                               ACT.Copy, scale=1.0 / (KS * WS)).then_inc(sems["v"], 1)

        def gram(e, eng, q, p, g):
            if e == "pe":
                done(eng, "e", q)
                need(eng, "v", q, g + 1)
                for n in (2 * g, 2 * g + 1):
                    for h in range(H):
                        c0 = (n % 2) * D + h * C
                        for ez, xz in PARTS:
                            last = eng.matmul(pf[g][:, c0:c0 + C],
                                              E[p][:, h, :, :, ez, n].rearrange("p b i -> p (b i)"),
                                              xb[:, h, :, xz, n], start=(ez, xz) == PARTS[0],
                                              stop=(ez, xz) == PARTS[-1])
                last.then_inc(sems["gp"], 1)
            if e == "act":
                need(eng, "gp", q, g + 1)
                done(eng, "td", q - 1)
                eng.activation(gs[:, :, :, 2 * g:2 * g + 2].rearrange("p h j n -> p (h j) n"),
                               pf[g][:, :].rearrange("p (n c) -> p c n", n=2),
                               ACT.Copy, scale=1.0 / (KS * KS)).then_inc(sems["g"], 1)

        def spread_gram(e, eng, q, p):
            if e == "sp":
                needs(eng, ("g", q, None), ("gh", q - 1, None))
                eng.dma_start(scr_g.rearrange("b i h t -> (b i) (h t)"),
                              gs[:, :, :, :].rearrange("p h j n -> p (h j n)")).then_inc(sems["gd"], 16)
                needs(eng, ("gd", q, None), ("tf", q - 1, None))
                for b in range(B):
                    eng.dma_start(gh[H * b:H * (b + 1), :, :, :].rearrange("h i j n -> h i (j n)"),
                                  scr_g[b].rearrange("i h t -> h i t")).then_inc(sems["gh"], 16)

        def invert(e, eng, q, p, rows):
            if e == "dve":
                if rows[0] == 1:
                    done(eng, "gh", q)
                    done(eng, "t16", q - 1)
                    eng.tensor_tensor(gh[:, :, :, :], gh[:, :, :, :],
                                      nmask[:, :, :, None].to_broadcast([P, C, C, NW]), ALU.mult)\
                       .then_inc(sems["tf"], 1)
                for i in rows:
                    need(eng, "tf", q, 2 * i - 1)
                    eng.tensor_tensor(tmp[:, 0:i, 0:i, :], tt[:, 0:i, 0:i, :],
                                      gh[:, i:i + 1, 0:i, :].to_broadcast([P, i, i, NW]), ALU.mult)\
                       .then_inc(sems["tf"], 1)
                    need(eng, "tf", q, 2 * i)
                    eng.tensor_reduce(tt[:, 0:i, i, :], tmp[:, 0:i, 0:i, :].rearrange("p m j n -> p m n j"), AX.X, ALU.add)\
                       .then_inc(sems["tf"], 1)

        def store_inverse(e, eng, q, p):
            src = tt[:, :, :, :].rearrange("p j i n -> p (j i) n")
            dst = t16[:, :, :, :, :].rearrange("p j i z n -> p (j i) z n")
            if e == "act":
                done(eng, "tf", q)
                eng.activation(dst[:, :, 0, :], src, ACT.Copy, scale=TS).then_inc(sems["t16h"], 1)
            if e == "dve":
                done(eng, "t16h", q)
                eng.scalar_tensor_tensor(dst[:, :, 1, :], src, TS, dst[:, :, 0, :], ALU.mult, ALU.subtract)\
                   .then_inc(sems["t16"], 1)
            if e == "sp":
                needs(eng, ("t16", q, None), ("tb", q - 1, None))
                eng.dma_start(scr_t.rearrange("b h j t -> (b h) (j t)"),
                              t16[:, :, :, :, :].rearrange("p j i z n -> p (j i z n)")).then_inc(sems["td"], 16)

        def load_inverse(e, eng, q, p):
            if e == "sp":
                needs(eng, ("td", q, None), ("tp", q - 1, None))
                for b in range(B):
                    eng.dma_start(tb[C * b:C * (b + 1), :, b].rearrange("j h i z n -> j h (i z n)"), scr_t[b].rearrange("h j t -> j h t"))\
                       .then_inc(sems["tb"], 16)

        def load_kb(e, eng, q, g):
            if e == "sp":
                needs(eng, ("k16", q, 2 * g + 2), ("sp", q - 1, 2 * g + 2))
                for b in range(B):
                    rows = slice(C * b, C * (b + 1))
                    eng.dma_start(kb[g][rows, b].rearrange("i k z h m -> i (k z h m)"),
                                  k16[rows, g].rearrange("i k z h m -> i (k z h m)")).then_inc(sems[f"kb{g}"], 16)

        def products(eng, stationary, moving):
            for h in range(H):
                for a, b in PARTS:
                    last = eng.matmul(pc[:, h * DH:(h + 1) * DH], stationary(h, a), moving(b)[:, h * DH:(h + 1) * DH],
                                      start=(a, b) == PARTS[0], stop=(a, b) == PARTS[-1])
            return last

        def split(eng, q, w, src, scale, dst, hi, lo):
            eng.tensor_scalar(dst[:, 0, :], src, scale, None, ALU.mult).then_inc(sems[hi], 1)
            need(eng, hi, q, w + 1)
            eng.scalar_tensor_tensor(dst[:, 1, :], src, scale, dst[:, 0, :], ALU.mult, ALU.subtract)\
               .then_inc(sems[lo], 1)

        def chain_k(e, eng, q, p, w):
            if e == "pe":
                need(eng, "s", q, w)
                products(eng, lambda h, z: E[p][:, h, :, :, z, w].rearrange("p b i -> p (b i)"),
                         lambda z: S16[:, z, :]).then_inc(sems["kp"], 1)
            if e == "dve":
                need(eng, "kp", q, w + 1)
                need(eng, "v", q, w // 2 + 1)
                eng.scalar_tensor_tensor(R[:, :], pc[:, 0:D], dcol[:, 0:1], v[:, p, w, :],
                                         ALU.mult, ALU.add).then_inc(sems["r0"], 1)
                need(eng, "r0", q, w + 1)
                split(eng, q, w, R[:, :], RS, R16, "rh", "r")

        def chain_t(e, eng, q, p, w):
            if e == "pe":
                need(eng, "r", q, w + 1)
                done(eng, "tb", q)
                products(eng, lambda h, z: tb[:, h, :, :, z, w].rearrange("p b i -> p (b i)"),
                         lambda z: R16[:, z, :]).then_inc(sems["tp"], 1)
            if e == "dve":
                need(eng, "tp", q, w + 1)
                need(eng, "y0", q, w - 1)
                split(eng, q, w, pc[:, 0:D], 1.0 / TS, U16[:, w % 2], "uh", "u")

        def chain_s(e, eng, q, p, w):
            if e == "dve":
                need(eng, "s0", q, w)
                eng.tensor_scalar(Sl[:, :], S[:, :], powers[:, C:C + 1], None, ALU.mult).then_inc(sems["sl"], 1)
            if e == "pe":
                need(eng, "u", q, w + 1)
                done(eng, f"kb{w // 2}", q)
                products(eng, lambda h, z: kb[w // 2][:, :, :, z, h, w % 2].rearrange("p b k -> p (b k)"),
                         lambda z: U16[:, w % 2, z, :]).then_inc(sems["sp"], 1)
            if e == "dve":
                need(eng, "sp", q, w + 1)
                need(eng, "sl", q, w + 1)
                eng.scalar_tensor_tensor(S[:, :], pc[:, 0:D], sc[:, BETAS:BETAS + 1], Sl[:, :],
                                         ALU.mult, ALU.add).then_inc(sems["s0"], 1)
                need(eng, "s0", q, w + 1)
                split(eng, q, w, S[:, :], SS, S16, "sh", "s")

        def attention_out(e, eng, q, p, w):
            if e == "pool":
                need(eng, "u", q, w + 1)
                done(eng, "nb", q)
                done(eng, "res", q - 1)
                eng.tensor_tensor(y[:, w, :], U16[:, w % 2, 0, :], U16[:, w % 2, 1, :], ALU.add)\
                   .then_inc(sems["y0"], 1)
                need(eng, "y0", q, w + 1)
                eng.tensor_tensor(y[:, w, :].rearrange("p (h d) -> p h d", h=H),
                                  y[:, w, :].rearrange("p (h d) -> p h d", h=H),
                                  nb[:, p, w, :, None].to_broadcast([P, H, DH]), ALU.mult)\
                   .then_inc(sems["y1"], 1)
            if e == "dve":
                need(eng, "y1", q, w + 1)
                eng.scalar_tensor_tensor(y[:, w, :], v[:, p, w, :], 2.0, y[:, w, :],
                                         ALU.mult, ALU.add).then_inc(sems["y"], 1)

        def load_residual(e, eng, q):
            if e == "sp":
                at = steps_of(eng, q)
                done(eng, "out", q - 1)
                for n in range(NW):
                    eng.dma_start(xr[:, n, :], x[:, bass.ds(at[n], C), :]).then_inc(sems["xr"], 16)
            if e == "pool":
                done(eng, "xr", q)
                eng.tensor_tensor(xr[:, :, :], xr[:, :, :], lnb[:, None, :].to_broadcast([P, NW, D]), ALU.add)\
                   .then_inc(sems["xrb"], 1)

        def statistics(e, eng, q, z, src, ready, st, mv, rs, prev):
            if e == "dve":
                for n in range(NW):
                    ready(n)
                    eng.bn_stats(st[:, n, :], src[:, n, :]).then_inc(sems[f"bs{z}"], 1)
                done(eng, prev, q - 1)
                for n in range(NW):
                    if n == 0:
                        done(eng, f"bs{z}", q)
                        eng.memset(carrier[:, :], 0.0)
                    eng.bn_aggr(mv[:, n, :], st[:, n, :]).then_inc(sems[f"ba{z}"], 1)
            if e == "pool":
                done(eng, f"ba{z}", q)
                done(eng, prev, q - 1)
                eng.tensor_tensor(rs[:, :], mv[:, :, 1], eps[:, :], ALU.add).then_inc(sems[f"ve{z}"], 1)
                done(eng, f"ve{z}", q)
                eng.tensor_tensor(rs[:, :], rs[:, :], mhalf[:, :], ALU.pow).then_inc(sems[f"rs{z}"], 1)

        def normalise(e, eng, q, z, dst, src, mv, rs, name):
            if e == "dve":
                done(eng, f"rs{z}", q)
                for n in range(NW):
                    eng.tensor_scalar(dst[:, n, :], src[:, n, :], mv[:, n, 0:1], rs[:, n:n + 1],
                                      ALU.subtract, ALU.mult).then_inc(sems[name], 1)

        def attention_norm(e, eng, q, p):
            statistics(e, eng, q, 1, y, lambda n: done(eng, "y", q), st1, mv1, rs1, "yn")
            normalise(e, eng, q, 1, y, y, mv1, rs1, "yn")
            if e == "pool":
                done(eng, "yn", q)
                eng.tensor_tensor(y[:, :, :], y[:, :, :], gamma[:, None, :].to_broadcast([P, NW, D]), ALU.mult)\
                   .then_inc(sems["yg"], 1)
            if e == "dve":
                done(eng, "yg", q)
                done(eng, "xrb", q)
                eng.tensor_tensor(xr[:, :, :], xr[:, :, :], y[:, :, :], ALU.add).then_inc(sems["res"], 1)

        def first_norm(e, eng, q):
            statistics(e, eng, q, 2, xr, lambda n: done(eng, "res", q), st2, mv2, rs2, "x1")
            normalise(e, eng, q, 2, xr, xr, mv2, rs2, "x1")

        def transpose_x1(e, eng, q):
            if e == "pe":
                done(eng, "x1", q)
                for half in range(2):
                    done(eng, "si", q - 1)
                    for n in range(NW):
                        last = eng.transpose(pg[half][:, n * P:(n + 1) * P], xr[:, n, half * P:(half + 1) * P],
                                             ident[:, :])
                    last.then_inc(sems["x1p"], 1)
            for half in range(2):
                if e == "act":
                    need(eng, "x1p", q, half + 1)
                    if not is_last(q):
                        done(eng, "vp", q + 2)
                        done(eng, "xtd", q + 2)
                    eng.activation(x1hi[:, half, :], pg[half][:, :], ACT.Copy, scale=XS).then_inc(sems["x1h"], 1)
                if e == "dve":
                    need(eng, "x1h", q, half + 1)
                    eng.scalar_tensor_tensor(x1lo[:, half, :], pg[half][:, :], XS, x1hi[:, half, :],
                                             ALU.mult, ALU.subtract).then_inc(sems["x1l"], 1)

        def hidden(e, eng, q, t):
            k = t % 2
            if e == "pe":
                done(eng, "x1l", q)
                if t >= 2:
                    need(eng, "h", q, t - 1)
                for bank, wt in ((pg[k], wg_t), (pu[k], wu_t)):
                    for half in range(2):
                        for part, xp in enumerate((x1hi, x1lo)):
                            last = eng.matmul(bank[:, :], wt[:, half, t * P:(t + 1) * P], xp[:, half, :],
                                              start=half + part == 0, stop=half + part == 2)
                last.then_inc(sems["gu"], 1)
            if e == "act":
                need(eng, "gu", q, t + 1)
                need(eng, "hl", q, t - 1)
                if t == 0 and not is_last(q):
                    done(eng, "nr", q + 2)
                eng.activation(gate[:, k, :], pg[k][:, :], ACT.Silu, scale=W_SCALE / XS).then_inc(sems["si"], 1)
            if e == "dve":
                need(eng, "si", q, t + 1)
                eng.scalar_tensor_tensor(gate[:, k, :], pu[k][:, :], W_SCALE * HS / XS, gate[:, k, :],
                                         ALU.mult, ALU.mult).then_inc(sems["h"], 1)
            if e == "act":
                need(eng, "h", q, t + 1)
                done(eng, "dn", q - 1)
                eng.activation(hhi[:, t, :], gate[:, k, :], ACT.Copy).then_inc(sems["hh"], 1)
            if e == "dve":
                need(eng, "hh", q, t + 1)
                eng.tensor_tensor(hlo[:, t, :], gate[:, k, :], hhi[:, t, :], ALU.subtract).then_inc(sems["hl"], 1)

        def down(e, eng, q, g):
            if e == "pe":
                done(eng, "hl", q)
                need(eng, "r2", q, g)
                for n in (2 * g, 2 * g + 1):
                    for t in range(NHT):
                        for part, hp in enumerate((hhi, hlo)):
                            last = eng.matmul(pd[:, (n % 2) * D:(n % 2 + 1) * D], hp[:, t, n * P:(n + 1) * P],
                                              wd_t[:, t, :], start=t + part == 0, stop=t + part == NHT)
                last.then_inc(sems["dn"], 1)
            if e == "dve":
                need(eng, "dn", q, g + 1)
                eng.scalar_tensor_tensor(xr[:, 2 * g:2 * g + 2, :], pd[:, :].rearrange("p (n d) -> p n d", n=2),
                                         W_SCALE / HS, xr[:, 2 * g:2 * g + 2, :], ALU.mult, ALU.add)\
                   .then_inc(sems["r2"], 1)

        def last_norm(e, eng, q):
            statistics(e, eng, q, 3, xr, lambda n: need(eng, "r2", q, n // 2 + 1), st3, mv3, rs3, "o")
            normalise(e, eng, q, 3, xr, xr, mv3, rs3, "o")

        def store_out(e, eng, q):
            if e == "sp":
                at = steps_of(eng, q)
                for n in range(NW):
                    need(eng, "o", q, n + 1)
                    eng.dma_start(out[:, bass.ds(at[n], C), :], xr[:, n, :]).then_inc(sems["out"], 16)

        def step(e, eng, s, p, chain=True, front=True, post=True):
            f, o_ = s + 1, s - 1
            fp, op = 1 - p, 1 - p

            def at(w, c):
                if chain:
                    (chain_k, chain_t, chain_s)[c](e, eng, s, p, w)
                    if c == 2:
                        attention_out(e, eng, s, p, w)

            if chain:
                load_inverse(e, eng, s, p)
            if post:
                load_residual(e, eng, o_)
            at(0, 0)
            if front:
                activate(e, eng, f, fp)
                spread_keys(e, eng, f, fp)
                key_norms(e, eng, f, fp)
            if chain:
                load_kb(e, eng, s, 1)
            at(0, 1)
            if front:
                static_out(e, eng, f, fp, 0)
            if post:
                attention_norm(e, eng, o_, op)
            at(0, 2)
            if front:
                static_out(e, eng, f, fp, 1)
            if post:
                first_norm(e, eng, o_)
            at(1, 0)
            if front:
                gram(e, eng, f, fp, 0)
            at(1, 1)
            if front:
                gram(e, eng, f, fp, 1)
                spread_gram(e, eng, f, fp)
            at(1, 2)
            if post:
                transpose_x1(e, eng, o_)
            at(2, 0)
            if post:
                hidden(e, eng, o_, 0)
            if front:
                invert(e, eng, f, fp, range(1, 7))
            at(2, 1)
            if post:
                hidden(e, eng, o_, 1)
            if front:
                invert(e, eng, f, fp, range(7, 10))
            if front:
                scale_keys(e, eng, f)
                load_kb(e, eng, f, 0)
                if not (isinstance(s, int) and s >= NS - 2):
                    load_x(e, eng, f + 1)
            at(2, 2)
            if post:
                hidden(e, eng, o_, 2)
            if front:
                invert(e, eng, f, fp, range(10, 12))
            at(3, 0)
            if post:
                hidden(e, eng, o_, 3)
            if front:
                invert(e, eng, f, fp, range(12, 14))
            at(3, 1)
            if post:
                hidden(e, eng, o_, 4)
            if front:
                invert(e, eng, f, fp, range(14, 16))
                store_inverse(e, eng, f, fp)
            at(3, 2)
            if post:
                hidden(e, eng, o_, 5)
                down(e, eng, o_, 0)
                down(e, eng, o_, 1)
                last_norm(e, eng, o_)
                store_out(e, eng, o_)

        def program(e, eng):
            load_x(e, eng, 0)
            step(e, eng, -1, 1, chain=False, post=False)
            step(e, eng, 0, 0, post=False)
            step(e, eng, 1, 1)
            with eng.Fori(1, NS // 2 - 1) as i:
                step(e, eng, i * 2, 0)
                step(e, eng, i * 2 + 1, 1)
            step(e, eng, NS - 2, 0)
            step(e, eng, NS - 1, 1, front=False)
            step(e, eng, NS, 0, chain=False, front=False)
            if e == "sp":
                done(eng, "out", NS - 1)

        as_u32 = lambda a: a.bitcast(mybir.dt.uint32)
        block = ctx.enter_context(nc.Block())
        w_nat = v[:, 0, 0:2, :]
        wg_nat = E[1][:, 0:4].rearrange("p h b i z n -> p (h b i z n)").bitcast(I32)[:, 0:NHT * D]\
            .rearrange("p (t d) -> p t d", t=NHT)
        wu_nat = E[1][:, 4:8].rearrange("p h b i z n -> p (h b i z n)").bitcast(I32)[:, 0:NHT * D]\
            .rearrange("p (t d) -> p t d", t=NHT)
        wd_nat = E[1][:, 8:12].rearrange("p h b i z n -> p (h b i z n)").bitcast(I32)[:, 0:2 * HID]\
            .rearrange("p (t d) -> p t d", t=2)
        wg16 = tb[:, 0:2].rearrange("p h b i z n -> p (h b i z n)")[:, 0:NHT * D]\
            .rearrange("p (t d) -> p t d", t=NHT)
        wu16 = tb[:, 2:4].rearrange("p h b i z n -> p (h b i z n)")[:, 0:NHT * D]\
            .rearrange("p (t d) -> p t d", t=NHT)
        wd16 = tb[:, 4:6].rearrange("p h b i z n -> p (h b i z n)")[:, 0:2 * HID]\
            .rearrange("p (t d) -> p t d", t=2)
        ps16 = [pg[0][:, 0:256].bitcast(F16), pg[1][:, 0:256].bitcast(F16)]

        jobs = []
        for dst, src in ((wg_t, wg16), (wu_t, wu16)):
            for half in range(2):
                for t0 in range(0, NHT, 2):
                    jobs.append(([src[:, t0 + a, half * P:(half + 1) * P] for a in range(2)],
                                 dst[:, half, t0 * P:(t0 + 2) * P]))
        for t in range(NHT):
            jobs.append(([wd16[:, a, t * P:(t + 1) * P] for a in range(2)], wd_t[:, t, :]))
        NJ = len(jobs)
        N_SETUP = 4 + 1 + 8 + 2 * C + 7 + 1 + (C - 1) + 1 + C

        @block.sync
        def _(eng):
            bc = lambda a, n: a.rearrange("(o n) -> o n", o=1).to_broadcast([P, n])
            eng.dma_start(sc[:, ETA:ETA + 1], eta.to_broadcast([P, 1])).then_inc(s_ld, 16)
            eng.dma_start(sc[:, LOGIT:LOGIT + 1], lam_logit.to_broadcast([P, 1])).then_inc(s_ld, 16)
            eng.dma_start(w_nat, W.rearrange("(a p) d -> p a d", p=P)).then_inc(s_ld, 16)
            eng.dma_start(wg_nat, w_gate.rearrange("(t p) d -> p t d", p=P)).then_inc(s_ld, 16)
            eng.dma_start(wu_nat, w_up.rearrange("(t p) d -> p t d", p=P)).then_inc(s_ld, 16)
            eng.dma_start(wd_nat, w_down.rearrange("(t p) d -> p t d", p=P)).then_inc(s_ld, 16)
            eng.dma_start(gamma[:, :], bc(ln_gamma, D)).then_inc(s_ld, 16)
            eng.dma_start(lnb[:, :], bc(ln_beta, D)).then_inc(s_ld, 16)
            eng.wait_ge(s_wt, NJ + 1)
            eng.wait_ge(s_pool0, 10)
            program("sp", eng)

        @block.gpsimd
        def _(eng):
            n = [0]
            chained(eng, eng.memset(ident[:, :], 0.0), n, s_pool0)
            chained(eng, eng.affine_select(out=ident[:, :], in_=ident[:, :], compare_op=ALU.not_equal, fill=1.0,
                                           base=0, pattern=[[-1, P]], channel_multiplier=1), n, s_pool0)
            chained(eng, eng.memset(mhalf[:, :], -0.5), n, s_pool0)
            chained(eng, eng.memset(eps[:, :], LN_EPS), n, s_pool0)
            chained(eng, eng.memset(as_u32(E[0][:, :, :, :, :, :].rearrange("p h b i z n -> p (h b i z n)")), 0), n, s_pool0)
            chained(eng, eng.memset(as_u32(kb[0][:, :, :, :, :, :].rearrange("p b k z h m -> p (b k z h m)")), 0), n, s_pool0)
            chained(eng, eng.memset(as_u32(kb[1][:, :, :, :, :, :].rearrange("p b k z h m -> p (b k z h m)")), 0), n, s_pool0)
            chained(eng, eng.memset(S[:, :], 0.0), n, s_pool0)
            eng.wait_ge(s_wt, NJ + 1)
            chained(eng, eng.memset(as_u32(E[1][:, :, :, :, :, :].rearrange("p h b i z n -> p (h b i z n)")), 0), n, s_pool0)
            chained(eng, eng.memset(as_u32(tb[:, :, :, :, :, :].rearrange("p h b i z n -> p (h b i z n)")), 0), n, s_pool0)
            eng.wait_ge(s_c, N_SETUP)
            program("pool", eng)

        @block.scalar
        def _(eng):
            eng.wait_ge(s_ld, 16 * 8)
            eng.activation(sc[:, OML:OML + 1], sc[:, LOGIT:LOGIT + 1], ACT.Sigmoid, scale=-1.0).then_inc(s_a0, 1)
            program("act", eng)

        @block.vector
        def _(eng):
            n = [0]

            def link(ins):
                chained(eng, ins, n, s_c)

            eng.wait_ge(s_pool0, 2)
            link(eng.tensor_copy(ident16[:, :], ident[:, :]))
            eng.wait_ge(s_ld, 16 * 8)
            link(eng.tensor_copy(wg16, wg_nat))
            link(eng.tensor_copy(wu16, wu_nat))
            link(eng.tensor_copy(wd16, wd_nat))
            n_w = n[0]
            for j, (_, dst) in enumerate(jobs):
                eng.wait_ge(s_ps, j + 1)
                eng.tensor_copy(dst, ps16[j % 2][:, 0:2 * P]).then_inc(s_wt, 1)
            eng.wait_ge(s_ps, NJ + 1)
            w_ps = pu[0][:, :].rearrange("p (a d) -> p a d", a=2)
            link(eng.tensor_scalar(w_t[:, :, 0, :], w_ps, WS, None, ALU.mult))
            eng.scalar_tensor_tensor(w_t[:, :, 1, :], w_ps, WS, w_t[:, :, 0, :], ALU.mult, ALU.subtract)\
               .then_inc(s_wt, 1)
            eng.wait_ge(s_a0, 1)
            link(eng.tensor_scalar(sc[:, LAM:LAM + 1], sc[:, OML:OML + 1], -1.0, 1.0, ALU.mult, ALU.add))
            link(eng.tensor_tensor(sc[:, BETA:BETA + 1], sc[:, ETA:ETA + 1], sc[:, OML:OML + 1], ALU.mult))
            link(eng.tensor_scalar(sc[:, BETA:BETA + 1], sc[:, BETA:BETA + 1], 1.0 / DH, None, ALU.mult))
            link(eng.tensor_scalar(sc[:, NBETA:NBETA + 1], sc[:, BETA:BETA + 1], -1.0, None, ALU.mult))
            link(eng.tensor_scalar(sc[:, BETAS:BETAS + 1], sc[:, BETA:BETA + 1], 1.0 / (KS * RS), None, ALU.mult))
            link(eng.tensor_scalar(sc[:, BETAR:BETAR + 1], sc[:, BETA:BETA + 1], 1.0 / RS, None, ALU.mult))
            link(eng.memset(powers[:, 0:1], 1.0))
            link(eng.memset(S16[:, :, :], 0.0))
            for m in range(C):
                link(eng.tensor_scalar(powers[:, m + 1:m + 2], powers[:, m:m + 1], sc[:, LAM:LAM + 1], None,
                                       ALU.mult))
            for m in range(C):
                link(eng.tensor_copy(rpowers[:, m:m + 1], powers[:, C - 1 - m:C - m]))
            link(eng.tensor_reduce(step_of[:, :], ident[:, :].rearrange("p (b i) -> p i b", b=B), AX.X, ALU.add))
            link(eng.tensor_tensor(ctmp[:, 0, :], step_of[:, :], powers[:, 1:C + 1], ALU.mult))
            link(eng.tensor_tensor(ctmp[:, 1, :], step_of[:, :], rpowers[:, :], ALU.mult))
            link(eng.tensor_reduce(dcol[:, :], ctmp[:, 0, :], AX.X, ALU.add))
            link(eng.tensor_scalar(dcol[:, :], dcol[:, :], -1.0 / (KS * SS), None, ALU.mult))
            link(eng.tensor_reduce(kcol[:, :], ctmp[:, 1, :], AX.X, ALU.add))
            link(eng.tensor_scalar(kcol[:, :], kcol[:, :], KS, None, ALU.mult))
            link(eng.memset(nmask[:, :, :], 0.0))
            flat = nmask[:, :, :].rearrange("p i j -> p (i j)")
            for d in range(1, C):
                link(eng.tensor_scalar(flat[:, C * d:C * C:C + 1],
                                       powers[:, d:d + 1].to_broadcast([P, C - d]),
                                       sc[:, NBETA:NBETA + 1], None, ALU.mult))
            link(eng.memset(tt[:, :, :, :], 0.0))
            for j in range(C):
                link(eng.memset(tt[:, j, j, :], 1.0))
            assert n[0] == N_SETUP
            program("dve", eng)

        @block.tensor
        def _(eng):
            eng.wait_ge(s_pool0, 2)
            eng.wait_ge(s_c, 4)
            for j, (srcs, _) in enumerate(jobs):
                if j >= 2:
                    eng.wait_ge(s_wt, j - 1)
                for a, src in enumerate(srcs):
                    last = eng.transpose(ps16[j % 2][:, a * P:(a + 1) * P], src, ident16[:, :])
                last.then_inc(s_ps, 1)
            for half in range(2):
                for a in range(2):
                    last = eng.transpose(pu[0][:, half * D + a * P:half * D + (a + 1) * P],
                                         w_nat[:, a, half * P:(half + 1) * P], ident[:, :])
            last.then_inc(s_ps, 1)
            eng.wait_ge(s_wt, NJ + 1)
            program("pe", eng)


_INS = ['L0_attn_x', 'L0_attn_W', 'L0_attn_ln_gamma', 'L0_attn_ln_beta', 'L0_attn_eta', 'L0_attn_lam_logit',
        'L0_ffn_w_gate', 'L0_ffn_w_up', 'L0_ffn_w_down']


def kernel(**inputs):
    import numpy as _np
    import concourse.bacc as _bacc
    from concourse.bass_utils import run_bass_kernel_spmd as _run

    nc = _bacc.Bacc("TRN2", target_bir_lowering=False, num_devices=1)
    arrays, args = {}, []
    for name in _INS:
        a = _np.ascontiguousarray(inputs[name])
        if a.ndim == 0:
            a = a.reshape(1)
        arrays[name] = a
        args.append(nc.dram_tensor(name, a.shape, mybir.dt.from_np(a.dtype), kind="ExternalInput").ap())
    args.append(nc.dram_tensor("y_out", (B, L, D), F32, kind="ExternalOutput").ap())
    build(nc, *args)
    r = _run(nc, [arrays], core_ids=[0])
    return r.results[0]["y_out"]
```

```python
from contextlib import ExitStack

import concourse.bass as bass
from concourse import mybir

F32 = mybir.dt.float32
F16 = mybir.dt.float16
I32 = mybir.dt.int32
ALU = mybir.AluOpType
ACT = mybir.ActivationFunctionType
AX = mybir.AxisListType

P = 128
B, L, D = 8, 2048, 256
H, DH = 16, 16
C = P // B
NW = 4
T = NW * C
NS = L // T
TOK = NW * P
HID = 768
NHT = HID // P
LN_EPS = 1e-5
W_SCALE = 1.0 / 127.0
XS = 2048.0
WS = 1024.0
KS = 4096.0
TS = 256.0
RS = 64.0
SS = 1024.0
HS = 0.25


def build(nc, x, W, ln_gamma, ln_beta, eta, lam_logit, w_gate, w_up, w_down, out):
    ctx = ExitStack()
    with ctx:
        def sb(name, shape, dt=F32):
            return ctx.enter_context(nc.sbuf_tensor(name, shape, dt))

        def sem(name):
            return ctx.enter_context(nc.semaphore(name))

        ident = sb("ident", [P, P])
        ident16 = sb("ident16", [P, P], F16)
        w_t = sb("w_t", [P, 2, 2, D], F16)
        wg_t = sb("wg_t", [P, 2, HID], F16)
        wu_t = sb("wu_t", [P, 2, HID], F16)
        wd_t = sb("wd_t", [P, NHT, D], F16)
        gamma = sb("gamma", [P, D])
        lnb = sb("lnb", [P, D])
        sc = sb("sc", [P, 8])
        ETA, LOGIT, OML, LAM, BETA, NBETA, BETAS, BETAR = range(8)
        powers = sb("powers", [P, C + 1])
        rpowers = sb("rpowers", [P, C])
        step_of = sb("step_of", [P, C])
        ctmp = sb("ctmp", [P, 2, C])
        dcol = sb("dcol", [P, 1])
        kcol = sb("kcol", [P, 1])
        nmask = sb("nmask", [P, C, C])
        mhalf = sb("mhalf", [P, NW])
        minus = sb("minus", [P, NW])
        eps = sb("eps", [P, NW])
        epsq = sb("epsq", [P, NW])
        carrier = sb("carrier", [P, 1])

        xa = sb("xa", [P, NW, D])
        k16 = sb("k16", [P, 2, DH, 2, H, 2], F16)
        nb = sb("nb", [P, 2, NW, H])
        xt = sb("xt", [P, 2, B, C, 2, NW], F16)
        E = [sb(f"e{p}", [P, H, B, C, 2, NW], F16) for p in range(2)]
        gs = sb("gs", [P, H, C, NW])
        gh = sb("gh", [P, C, C, NW])
        xb = gh[:, :, :, :].rearrange("p i j n -> p (i j n)").bitcast(F16)\
            .rearrange("p (h i z n) -> p h i z n", h=H, i=C, z=2)
        tt = sb("tt", [P, C, C, NW])
        tmp = gs[:, 0:C - 1, :, :]
        t16 = gs[:, :, :, :].rearrange("p h j n -> p (h j n)").bitcast(F16)\
            .rearrange("p (j i z n) -> p j i z n", j=C, i=C, z=2)
        tb = sb("tb", [P, H, B, C, 2, NW], F16)
        kb = [sb(f"kb{g}", [P, B, DH, 2, H, 2], F16) for g in range(2)]
        v = sb("v", [P, 2, NW, D])
        S = sb("S", [P, D])
        S16 = sb("S16", [P, 2, D], F16)
        R = sb("R", [P, D])
        R16 = sb("R16", [P, 2, D], F16)
        U16 = sb("U16", [P, 2, 2, D], F16)
        bu = sb("bu", [P, D])
        xr = sb("xr", [P, NW, D])
        st1 = sb("st1", [P, NW, 6])
        mv1 = sb("mv1", [P, NW, 2])
        rs1 = sb("rs1", [P, NW])
        nm1 = sb("nm1", [P, NW])
        st2 = sb("st2", [P, NW, 6])
        mv2 = sb("mv2", [P, NW, 2])
        rs2 = sb("rs2", [P, NW])
        nm2 = sb("nm2", [P, NW])
        st3 = sb("st3", [P, NW, 6])
        mv3 = sb("mv3", [P, NW, 2])
        rs3 = sb("rs3", [P, NW])
        nm3 = sb("nm3", [P, NW])
        x1hi = sb("x1hi", [P, 2, TOK], F16)
        x1lo = sb("x1lo", [P, 2, TOK], F16)
        gate = sb("gate", [P, 2, TOK])
        res = gate[:, :, :].rearrange("p k (n d) -> p (k n) d", d=D)
        hhi = sb("hhi", [P, NHT, TOK], F16)
        hlo = sb("hlo", [P, NHT, TOK], F16)
        sq = hhi[:, 0:4, :].rearrange("p t m -> p (t m)").bitcast(F32)\
            .rearrange("p (n d) -> p n d", n=NW)

        pc = ctx.enter_context(nc.psum_tensor("pc", [P, 512], F32))
        pf = [ctx.enter_context(nc.psum_tensor(f"pf{i}", [P, 512], F32)) for i in range(2)]
        pg = [ctx.enter_context(nc.psum_tensor(f"pg{i}", [P, 512], F32)) for i in range(2)]
        pu = [ctx.enter_context(nc.psum_tensor(f"pu{i}", [P, 512], F32)) for i in range(2)]
        pd = ctx.enter_context(nc.psum_tensor("pd", [P, 512], F32))

        scr_x = nc.dram_tensor("scr_x", [2, P, B, 2 * T], F16).ap()
        scr_g = nc.dram_tensor("scr_g", [B, C, H, T], F32).ap()
        scr_t = nc.dram_tensor("scr_t", [B, H, C, 2 * T], F16).ap()

        names = dict(
            xin=64, xa=1, k16h=4, k16=4, sq=1, nr=1, nb=1,
            xtp=2, xth=2, xt=2, vp=2, v=2,
            xtd=32, e=256, gp=2, g=2, gd=16, gh=128,
            tf=29, tc=1, t1=1, t16h=1, t16=1, td=16, tb=128,
            kb0=128, kb1=128,
            kp=4, r0=4, rh=4, r=4, tp=4, uh=4, u=4, sp=4, s0=4, sh=4, s=4, sl=4, y0=4, y1=4, y=4,
            xr=64, xrb=1, bs1=4, ba1=4, mm1=1, ve1=1, rs1=1, nm1=1, yn=4, yg=1, res=1,
            bs2=4, ba2=4, mm2=1, ve2=1, rs2=1, nm2=1, x1=4, x1p=2, x1h=2, x1l=2,
            gu=6, si=6, h=6, hh=6, hl=6, dn=2, r2=2,
            bs3=4, ba3=4, mm3=1, ve3=1, rs3=1, nm3=1, o=4, out=64)
        sems = {n: sem("s_" + n) for n in names}
        s_ld = sem("s_ld")
        s_hop = sem("s_hop")
        s_pool0 = sem("s_pool0")
        s_c = sem("s_c")
        s_a0 = sem("s_a0")
        s_ps = sem("s_ps")
        s_wt = sem("s_wt")

        def needs(eng, *events):
            values = []
            for name, q, k in events:
                k = names[name] if k is None else k
                if k <= 0:
                    q, k = q - 1, k + names[name]
                if isinstance(q, int):
                    if q >= 0:
                        values.append((name, q * names[name] + k))
                else:
                    values.append((name, eng.snap(q * names[name] + k)))
            for name, value in values:
                eng.wait_ge(sems[name], value)
                if eng.engine == mybir.EngineType.SP and (name, value) != values[-1]:
                    eng.sem_inc(s_hop, 1)

        def need(eng, name, q, k):
            needs(eng, (name, q, k))

        def done(eng, name, q):
            needs(eng, (name, q, None))

        def is_last(q):
            return isinstance(q, int) and q + 2 >= NS

        def steps_of(eng, q):
            return [q * T + n * C if isinstance(q, int) else eng.snap(q * T + n * C) for n in range(NW)]

        def chained(eng, ins, counter, semaphore):
            counter[0] += 1
            ins.then_inc(semaphore, 1)
            eng.wait_ge(semaphore, counter[0])

        PARTS = [(0, 0), (0, 1), (1, 0), (1, 1)]
        PARTS3 = [(half, a, b) for half in range(2) for a, b in PARTS]

        def load_x(e, eng, q):
            if e == "sp":
                at = steps_of(eng, q)
                needs(eng, ("xtp", q - 1, None), ("sq", q - 1, None), ("k16", q - 1, None))
                for n in range(NW):
                    eng.dma_start(xa[:, n, :], x[:, bass.ds(at[n], C), :]).then_inc(sems["xin"], 16)

        def activate(e, eng, q):
            if e == "act":
                done(eng, "xin", q)
                eng.activation(xa[:, :, :], xa[:, :, :], ACT.Tanh).then_inc(sems["xa"], 1)

        def square(e, eng, q):
            if e == "pool":
                done(eng, "xa", q)
                done(eng, "dn", q - 3)
                done(eng, "nr", q - 1)
                eng.tensor_tensor(sq, xa[:, :, :], xa[:, :, :], ALU.mult).then_inc(sems["sq"], 1)

        def transpose_keys(e, eng, q):
            if e == "pe":
                done(eng, "xa", q)
                done(eng, "v", q - 1)
                for half in range(2):
                    for n in range(NW):
                        last = eng.transpose(pf[half][:, n * P:(n + 1) * P], xa[:, n, half * P:(half + 1) * P],
                                             ident[:, :])
                    last.then_inc(sems["xtp"], 1)
            for half in range(2):
                src = pf[half][:, :].rearrange("p (n t) -> p t n", n=NW)
                dst = xt[:, half].rearrange("p b i z n -> p (b i) z n")
                if e == "act":
                    need(eng, "xtp", q, half + 1)
                    done(eng, "vp", q - 1)
                    done(eng, "xtd", q - 1)
                    eng.activation(dst[:, :, 0, :], src, ACT.Copy, scale=KS).then_inc(sems["xth"], 1)
                if e == "dve":
                    need(eng, "xth", q, half + 1)
                    eng.scalar_tensor_tensor(dst[:, :, 1, :], src, KS, dst[:, :, 0, :], ALU.mult, ALU.subtract)\
                       .then_inc(sems["xt"], 1)

        def scale_keys(e, eng, q):
            for g in range(2):
                src = xa[:, 2 * g:2 * g + 2, :].rearrange("p m (h k) -> p m k h", h=H)
                dst = k16[:, g].rearrange("p k z h m -> p z m k h")
                for m in range(2):
                    if e == "act":
                        if m == 0 and g == 0:
                            done(eng, "kb0", q - 1)
                            done(eng, "kb1", q - 1)
                        eng.activation(dst[:, 0, m], src[:, m], ACT.Copy, scale=kcol[:, 0:1])\
                           .then_inc(sems["k16h"], 1)
                    if e == "dve":
                        need(eng, "k16h", q, 2 * g + m + 1)
                        eng.scalar_tensor_tensor(dst[:, 1, m], src[:, m], kcol[:, 0:1], dst[:, 0, m],
                                                 ALU.mult, ALU.subtract).then_inc(sems["k16"], 1)

        def key_norms(e, eng, q, p):
            if e == "dve":
                done(eng, "y1", q - 2)
                done(eng, "sq", q)
                eng.tensor_reduce(nb[:, p, :, :], sq.rearrange("p n (h k) -> p n h k", h=H),
                                  AX.X, ALU.add).then_inc(sems["nr"], 1)
                done(eng, "nr", q)
                eng.tensor_scalar(nb[:, p, :, :], nb[:, p, :, :], sc[:, BETAR:BETAR + 1], -0.5 / RS,
                                  ALU.mult, ALU.add).then_inc(sems["nb"], 1)

        def store_keys(e, eng, q):
            if e == "sp":
                for half in range(2):
                    needs(eng, ("xt", q, half + 1), ("e", q - 1, None))
                    eng.dma_start(scr_x[half], xt[:, half].rearrange("p b i z n -> p b (i z n)"))\
                       .then_inc(sems["xtd"], 16)

        def spread_keys(e, eng, q, p):
            if e == "sp":
                src = scr_x.rearrange("z (h k) b t -> k (z h) b t", k=DH)
                needs(eng, ("xtd", q, None), ("kp", q - 2, None))
                for b in range(B):
                    eng.dma_start(E[p][DH * b:DH * (b + 1), :, b].rearrange("k h i z n -> k h (i z n)"),
                                  src[:, :, b, :]).then_inc(sems["e"], 16)

        def spread_packed_keys(e, eng, q):
            if e == "sp":
                src = scr_x.rearrange("z (h k) b t -> k (z h) b t", k=DH)
                done(eng, "tf", q - 1)
                for b in range(B):
                    eng.dma_start(xb[DH * b:DH * (b + 1)].rearrange("k h i z n -> k h (i z n)"),
                                  src[:, :, b, :]).then_inc(sems["e"], 16)

        def static_out(e, eng, q, p, g):
            if e == "pe":
                done(eng, "xt", q)
                need(eng, "g", q, g + 1)
                for n in (2 * g, 2 * g + 1):
                    for half, xz, wz in PARTS3:
                        last = eng.matmul(pf[g][:, (n % 2) * D:(n % 2 + 1) * D],
                                          xt[:, half, :, :, xz, n].rearrange("p b i -> p (b i)"),
                                          w_t[:, half, wz, :], start=(half, xz, wz) == PARTS3[0],
                                          stop=(half, xz, wz) == PARTS3[-1])
                last.then_inc(sems["vp"], 1)
            if e == "act":
                need(eng, "vp", q, g + 1)
                done(eng, "res", q - 2)
                done(eng, "out", q - 3)
                eng.activation(v[:, p, 2 * g:2 * g + 2, :], pf[g][:, :].rearrange("p (n d) -> p n d", n=2),
                               ACT.Copy, scale=1.0 / (KS * WS)).then_inc(sems["v"], 1)

        def gram(e, eng, q, p, g):
            if e == "pe":
                done(eng, "e", q)
                done(eng, "xt", q)
                for n in (2 * g, 2 * g + 1):
                    for h in range(H):
                        c0 = (n % 2) * D + h * C
                        for ez, xz in PARTS:
                            last = eng.matmul(pf[g][:, c0:c0 + C],
                                              E[p][:, h, :, :, ez, n].rearrange("p b i -> p (b i)"),
                                              xb[:, h, :, xz, n], start=(ez, xz) == PARTS[0],
                                              stop=(ez, xz) == PARTS[-1])
                last.then_inc(sems["gp"], 1)
            if e == "act":
                need(eng, "gp", q, g + 1)
                done(eng, "td", q - 1)
                eng.activation(gs[:, :, :, 2 * g:2 * g + 2].rearrange("p h j n -> p (h j) n"),
                               pf[g][:, :].rearrange("p (n c) -> p c n", n=2),
                               ACT.Copy, scale=1.0 / (KS * KS)).then_inc(sems["g"], 1)

        def store_gram(e, eng, q):
            if e == "sp":
                needs(eng, ("g", q, None), ("gh", q - 1, None))
                eng.dma_start(scr_g.rearrange("b i h t -> (b i) (h t)"),
                              gs[:, :, :, :].rearrange("p h j n -> p (h j n)")).then_inc(sems["gd"], 16)

        def load_gram(e, eng, q):
            if e == "sp":
                needs(eng, ("gd", q, None), ("tf", q - 1, None))
                for b in range(B):
                    eng.dma_start(gh[H * b:H * (b + 1), :, :, :].rearrange("h i j n -> h i (j n)"),
                                  scr_g[b].rearrange("i h t -> h i t")).then_inc(sems["gh"], 16)

        def mask_gram(e, eng, q):
            if e == "dve":
                done(eng, "gh", q)
                eng.tensor_tensor(gh[:, :, :, :], gh[:, :, :, :],
                                  nmask[:, :, :, None].to_broadcast([P, C, C, NW]), ALU.mult)\
                   .then_inc(sems["tf"], 1)
            if e == "act":
                need(eng, "tf", q, 1)
                done(eng, "t16", q - 1)
                eng.activation(tt[:, :, :, :], gh[:, :, :, :].rearrange("p i j n -> p j i n"), ACT.Copy)\
                   .then_inc(sems["tc"], 1)
            if e == "pool":
                done(eng, "tc", q)
                one = powers[:, 0:1, None].to_broadcast([P, C, NW])
                eng.tensor_tensor(tt[:, :, :, :].rearrange("p j i n -> p (j i) n")[:, 0:C * C:C + 1, :],
                                  one, one, ALU.mult).then_inc(sems["t1"], 1)

        def invert(e, eng, q, cols):
            if e == "dve":
                for j in cols:
                    m, i = slice(0, j), slice(j + 1, C)
                    if j == 1:
                        done(eng, "tc", q)
                    else:
                        need(eng, "tf", q, 2 * j - 1)
                    eng.tensor_tensor(tmp[:, m, 0:C - 1 - j, :],
                                      tt[:, m, j:j + 1, :].to_broadcast([P, j, C - 1 - j, NW]),
                                      gh[:, i, j, :][:, None].to_broadcast([P, j, C - 1 - j, NW]), ALU.mult)\
                       .then_inc(sems["tf"], 1)
                    need(eng, "tf", q, 2 * j)
                    eng.tensor_tensor(tt[:, m, i, :], tt[:, m, i, :], tmp[:, m, 0:C - 1 - j, :], ALU.add)\
                       .then_inc(sems["tf"], 1)

        def store_inverse(e, eng, q):
            src = tt[:, :, :, :].rearrange("p j i n -> p (j i) n")
            dst = t16[:, :, :, :, :].rearrange("p j i z n -> p (j i) z n")
            if e == "act":
                done(eng, "tf", q)
                done(eng, "t1", q)
                eng.activation(dst[:, :, 0, :], src, ACT.Copy, scale=TS).then_inc(sems["t16h"], 1)
            if e == "dve":
                done(eng, "t16h", q)
                eng.scalar_tensor_tensor(dst[:, :, 1, :], src, TS, dst[:, :, 0, :], ALU.mult, ALU.subtract)\
                   .then_inc(sems["t16"], 1)
            if e == "sp":
                needs(eng, ("t16", q, None), ("tb", q - 1, None))
                eng.dma_start(scr_t.rearrange("b h j t -> (b h) (j t)"),
                              t16[:, :, :, :, :].rearrange("p j i z n -> p (j i z n)")).then_inc(sems["td"], 16)

        def load_inverse(e, eng, q):
            if e == "sp":
                needs(eng, ("td", q, None), ("tp", q - 1, None))
                for b in range(B):
                    eng.dma_start(tb[C * b:C * (b + 1), :, b].rearrange("j h i z n -> j h (i z n)"), scr_t[b].rearrange("h j t -> j h t"))\
                       .then_inc(sems["tb"], 16)

        def load_kb(e, eng, q, g):
            if e == "sp":
                needs(eng, ("k16", q, 2 * g + 2), ("sp", q - 1, 2 * g + 2))
                for b in range(B):
                    rows = slice(C * b, C * (b + 1))
                    eng.dma_start(kb[g][rows, b].rearrange("i k z h m -> i (k z h m)"),
                                  k16[rows, g].rearrange("i k z h m -> i (k z h m)")).then_inc(sems[f"kb{g}"], 16)

        def products(eng, stationary, moving):
            for h in range(H):
                for a, b in PARTS:
                    last = eng.matmul(pc[:, h * DH:(h + 1) * DH], stationary(h, a), moving(b)[:, h * DH:(h + 1) * DH],
                                      start=(a, b) == PARTS[0], stop=(a, b) == PARTS[-1])
            return last

        def split(eng, q, w, src, scale, dst, hi, lo):
            eng.tensor_scalar(dst[:, 0, :], src, scale, None, ALU.mult).then_inc(sems[hi], 1)
            need(eng, hi, q, w + 1)
            eng.scalar_tensor_tensor(dst[:, 1, :], src, scale, dst[:, 0, :], ALU.mult, ALU.subtract)\
               .then_inc(sems[lo], 1)

        def chain_k(e, eng, q, p, w):
            if e == "pe":
                need(eng, "s", q, w)
                products(eng, lambda h, z: E[p][:, h, :, :, z, w].rearrange("p b i -> p (b i)"),
                         lambda z: S16[:, z, :]).then_inc(sems["kp"], 1)
            if e == "dve":
                need(eng, "kp", q, w + 1)
                need(eng, "v", q, w // 2 + 1)
                eng.scalar_tensor_tensor(R[:, :], pc[:, 0:D], dcol[:, 0:1], v[:, p, w, :],
                                         ALU.mult, ALU.add).then_inc(sems["r0"], 1)
                need(eng, "r0", q, w + 1)
                split(eng, q, w, R[:, :], RS, R16, "rh", "r")

        def chain_t(e, eng, q, p, w):
            if e == "pe":
                need(eng, "r", q, w + 1)
                done(eng, "tb", q)
                products(eng, lambda h, z: tb[:, h, :, :, z, w].rearrange("p b i -> p (b i)"),
                         lambda z: R16[:, z, :]).then_inc(sems["tp"], 1)
            if e == "dve":
                need(eng, "tp", q, w + 1)
                need(eng, "y0", q, w - 1)
                split(eng, q, w, pc[:, 0:D], 1.0 / TS, U16[:, w % 2], "uh", "u")

        def chain_s(e, eng, q, p, w):
            if e == "dve":
                need(eng, "s0", q, w)
                eng.tensor_scalar(S[:, :], S[:, :], powers[:, C:C + 1], None, ALU.mult).then_inc(sems["sl"], 1)
            if e == "pe":
                need(eng, "u", q, w + 1)
                done(eng, f"kb{w // 2}", q)
                products(eng, lambda h, z: kb[w // 2][:, :, :, z, h, w % 2].rearrange("p b k -> p (b k)"),
                         lambda z: U16[:, w % 2, z, :]).then_inc(sems["sp"], 1)
            if e == "dve":
                need(eng, "sp", q, w + 1)
                need(eng, "sl", q, w + 1)
                eng.scalar_tensor_tensor(S[:, :], pc[:, 0:D], sc[:, BETAS:BETAS + 1], S[:, :],
                                         ALU.mult, ALU.add).then_inc(sems["s0"], 1)
                need(eng, "s0", q, w + 1)
                split(eng, q, w, S[:, :], SS, S16, "sh", "s")

        def attention_out(e, eng, q, p, w):
            if e == "pool":
                need(eng, "u", q, w + 1)
                done(eng, "nb", q)
                need(eng, "y", q, w)
                eng.tensor_tensor(bu[:, :], U16[:, w % 2, 0, :], U16[:, w % 2, 1, :], ALU.add)\
                   .then_inc(sems["y0"], 1)
                need(eng, "y0", q, w + 1)
                eng.tensor_tensor(bu[:, :].rearrange("p (h d) -> p h d", h=H),
                                  bu[:, :].rearrange("p (h d) -> p h d", h=H),
                                  nb[:, p, w, :, None].to_broadcast([P, H, DH]), ALU.mult)\
                   .then_inc(sems["y1"], 1)
                need(eng, "y1", q, w + 1)
                eng.tensor_tensor(v[:, p, w, :], v[:, p, w, :], bu[:, :], ALU.add).then_inc(sems["y"], 1)

        def load_residual(e, eng, q):
            if e == "sp":
                at = steps_of(eng, q)
                done(eng, "hl", q - 1)
                for n in range(NW):
                    eng.dma_start(res[:, n, :], x[:, bass.ds(at[n], C), :]).then_inc(sems["xr"], 16)
            if e == "pool":
                done(eng, "xr", q)
                eng.tensor_tensor(res, res, lnb[:, None, :].to_broadcast([P, NW, D]), ALU.add)\
                   .then_inc(sems["xrb"], 1)

        def statistics(e, eng, q, z, src, ready, st, mv, rs, prev, nm, epsilon):
            if e == "dve":
                for n in range(NW):
                    ready(n)
                    eng.bn_stats(st[:, n, :], src[:, n, :]).then_inc(sems[f"bs{z}"], 1)
                done(eng, f"nm{z}", q - 1)
                for n in range(NW):
                    if n == 0:
                        done(eng, f"bs{z}", q)
                        eng.memset(carrier[:, :], 0.0)
                    eng.bn_aggr(mv[:, n, :], st[:, n, :]).then_inc(sems[f"ba{z}"], 1)
            if e == "pool":
                done(eng, f"ba{z}", q)
                done(eng, prev, q - 1)
                eng.tensor_tensor(nm[:, :], mv[:, :, 0], minus[:, :], ALU.mult).then_inc(sems[f"mm{z}"], 1)
                eng.tensor_tensor(rs[:, :], mv[:, :, 1], epsilon[:, :], ALU.add)\
                   .then_inc(sems[f"ve{z}"], 1)
                done(eng, f"ve{z}", q)
                eng.tensor_tensor(rs[:, :], rs[:, :], mhalf[:, :], ALU.pow).then_inc(sems[f"rs{z}"], 1)
                done(eng, f"rs{z}", q)
                eng.tensor_tensor(nm[:, :], nm[:, :], rs[:, :], ALU.mult).then_inc(sems[f"nm{z}"], 1)

        def normalise(e, eng, q, z, dst, src, nm, rs, name):
            if e == "act":
                done(eng, f"nm{z}", q)
                for n in range(NW):
                    eng.activation(dst[:, n, :], src[:, n, :], ACT.Identity, bias=nm[:, n:n + 1],
                                   scale=rs[:, n:n + 1]).then_inc(sems[name], 1)

        def attention_statistics(e, eng, q, p):
            statistics(e, eng, q, 1, v[:, p], lambda n: need(eng, "y", q, n + 1), st1, mv1, rs1, "yn", nm1, epsq)

        def attention_norm(e, eng, q, p):
            normalise(e, eng, q, 1, v[:, p], v[:, p], nm1, rs1, "yn")
            if e == "pool":
                done(eng, "yn", q)
                eng.tensor_tensor(v[:, p], v[:, p], gamma[:, None, :].to_broadcast([P, NW, D]), ALU.mult)\
                   .then_inc(sems["yg"], 1)
                done(eng, "yg", q)
                done(eng, "xrb", q)
                eng.tensor_tensor(res, res, v[:, p], ALU.add).then_inc(sems["res"], 1)

        def first_statistics(e, eng, q):
            statistics(e, eng, q, 2, res, lambda n: done(eng, "res", q), st2, mv2, rs2, "x1", nm2, eps)

        def first_norm(e, eng, q):
            if e == "act":
                done(eng, "o", q - 1)
            normalise(e, eng, q, 2, xr, res, nm2, rs2, "x1")

        def transpose_x1(e, eng, q):
            if e == "pe":
                done(eng, "x1", q)
                for half in range(2):
                    done(eng, "si", q - 1)
                    for n in range(NW):
                        last = eng.transpose(pg[half][:, n * P:(n + 1) * P], xr[:, n, half * P:(half + 1) * P],
                                             ident[:, :])
                    last.then_inc(sems["x1p"], 1)
            for half in range(2):
                if e == "act":
                    need(eng, "x1p", q, half + 1)
                    done(eng, "gu", q - 1)
                    eng.activation(x1hi[:, half, :], pg[half][:, :], ACT.Copy, scale=XS).then_inc(sems["x1h"], 1)
                if e == "dve":
                    need(eng, "x1h", q, half + 1)
                    eng.scalar_tensor_tensor(x1lo[:, half, :], pg[half][:, :], XS, x1hi[:, half, :],
                                             ALU.mult, ALU.subtract).then_inc(sems["x1l"], 1)

        def hidden(e, eng, q, t):
            k = t % 2
            if e == "pe":
                done(eng, "x1l", q)
                if t == 0:
                    done(eng, "r2", q - 1)
                if t >= 2:
                    need(eng, "h", q, t - 1)
                for bank, wt in ((pg[k], wg_t), (pu[k], wu_t)):
                    for half in range(2):
                        for part, xp in enumerate((x1hi, x1lo)):
                            last = eng.matmul(bank[:, :], wt[:, half, t * P:(t + 1) * P], xp[:, half, :],
                                              start=half + part == 0, stop=half + part == 2)
                last.then_inc(sems["gu"], 1)
            if e == "act":
                need(eng, "gu", q, t + 1)
                need(eng, "hl", q, t - 1)
                eng.activation(gate[:, k, :], pg[k][:, :], ACT.Silu, scale=W_SCALE / XS).then_inc(sems["si"], 1)

        def multiply(e, eng, q, t):
            k = t % 2
            if e == "dve":
                need(eng, "si", q, t + 1)
                eng.scalar_tensor_tensor(gate[:, k, :], pu[k][:, :], W_SCALE * HS / XS, gate[:, k, :],
                                         ALU.mult, ALU.mult).then_inc(sems["h"], 1)
            if e == "act":
                need(eng, "h", q, t + 1)
                if t == 0:
                    done(eng, "dn", q - 1)
                    if not is_last(q):
                        done(eng, "nr", q + 2)
                eng.activation(hhi[:, t, :], gate[:, k, :], ACT.Copy).then_inc(sems["hh"], 1)
            if e == "pool":
                need(eng, "hh", q, t + 1)
                eng.tensor_tensor(hlo[:, t, :], gate[:, k, :], hhi[:, t, :], ALU.subtract).then_inc(sems["hl"], 1)

        def down(e, eng, q, g, tiles):
            bank = (pd, pu[0])[g]
            if e == "pe":
                need(eng, "hl", q, tiles[-1] + 1)
                if tiles[0] == 0 and g == 0:
                    need(eng, "r2", q - 1, 1)
                if tiles[0] == 0 and g == 1:
                    need(eng, "h", q, NHT - 1)
                for n in (2 * g, 2 * g + 1):
                    for t in tiles:
                        for part, hp in enumerate((hhi, hlo)):
                            last = eng.matmul(bank[:, (n % 2) * D:(n % 2 + 1) * D], hp[:, t, n * P:(n + 1) * P],
                                              wd_t[:, t, :], start=n % 2 + t + part == 0, stop=n % 2 + t + part == NHT + 1)
                if tiles[-1] == NHT - 1:
                    last.then_inc(sems["dn"], 1)

        def add_ffn(e, eng, q, g):
            bank = (pd, pu[0])[g]
            if e == "dve":
                need(eng, "dn", q, g + 1)
                eng.scalar_tensor_tensor(xr[:, 2 * g:2 * g + 2, :], bank[:, :].rearrange("p (n d) -> p n d", n=2),
                                         W_SCALE / HS, xr[:, 2 * g:2 * g + 2, :], ALU.mult, ALU.add)\
                   .then_inc(sems["r2"], 1)

        def last_statistics(e, eng, q):
            statistics(e, eng, q, 3, xr, lambda n: need(eng, "r2", q, n // 2 + 1), st3, mv3, rs3, "o", nm3, eps)

        def last_norm(e, eng, q, p):
            if e == "act":
                if isinstance(q, int) and q == NS - 1:
                    done(eng, "out", q - 2)
                else:
                    done(eng, "res", q + 1)
            normalise(e, eng, q, 3, v[:, 1 - p], xr, nm3, rs3, "o")

        def store_out(e, eng, q, p):
            if e == "sp":
                at = steps_of(eng, q)
                for n in range(NW):
                    needs(eng, ("o", q, n + 1), *([("out", q - 1, None)] if n == 0 else []))
                    eng.dma_start(out[:, bass.ds(at[n], C), :], v[:, 1 - p, n, :]).then_inc(sems["out"], 16)

        def step(e, eng, s, p, chain=True, front=True, early=True, post=True, tail=True):
            f, a, o_, t_ = s + 1, s + 2, s - 1, s - 2
            fp, op = 1 - p, 1 - p
            slots = [[] for _ in range(3 * NW)]

            def put(slot, engines, stage, *args):
                if e in engines.split():
                    slots[slot].append(lambda: stage(e, eng, *args))

            if tail:
                put(0, "dve act pool", multiply, t_, NHT - 1)
            if front:
                put(10, "act", store_inverse, f)
            if chain:
                for w in range(NW):
                    for c, stage in enumerate((chain_k, chain_t, chain_s)):
                        put(3 * w + c, "dve pe", stage, s, p, w)
                for w in range(NW - 1):
                    put(3 * w + 2, "pool", attention_out, s, p, w)
            if post:
                put(0, "sp", load_residual, o_)
                put(0, "pool", attention_out, o_, op, NW - 1)
                put(0, "dve pool", attention_statistics, o_, op)
                put(0, "pool", load_residual, o_)
                put(0, "act pool", attention_norm, o_, op)
            if tail:
                put(0, "pe", down, t_, 1, range(4))
                put(1, "pe", down, t_, 0, range(4, NHT))
                put(1, "pe", down, t_, 1, range(4, NHT))
                put(1, "dve", add_ffn, t_, 0)
                put(1, "dve", add_ffn, t_, 1)
                put(1, "dve pool", last_statistics, t_)
            if front:
                put(0, "sp", spread_packed_keys, f)
            if chain:
                put(1, "sp", load_kb, s, 1)
            if post:
                put(2, "dve pool", first_statistics, o_)
            if front:
                put(2, "pe act", gram, f, fp, 0)
            if tail:
                put(3, "act", last_norm, t_, p)
            if front:
                put(3, "pe act", gram, f, fp, 1)
                put(3, "sp", store_gram, f)
            if post:
                put(3, "act", first_norm, o_)
            if tail:
                put(3, "sp", store_out, t_, p)
            if front:
                put(3, "sp", load_gram, f)
                put(2, "pool", square, f)
                put(3, "act dve", scale_keys, f)
                put(4, "pe", static_out, f, fp, 0)
            if post:
                put(4, "pe act dve", transpose_x1, o_)
            if front:
                put(4, "act", static_out, f, fp, 0)
                put(4, "dve", key_norms, f, fp)
            if early:
                put(5, "sp", load_x, a)
            if front:
                put(5, "sp", load_kb, f, 0)
                put(5, "dve act pool", mask_gram, f)
            for t in range(NHT):
                if post:
                    put(5 + t, "pe act", hidden, o_, t)
                    if t < NHT - 1:
                        put(6 + t, "dve act pool", multiply, o_, t)
            if front:
                put(5, "pe act", static_out, f, fp, 1)
                for t, cols in enumerate((range(1, 4), range(4, 7), range(7, 10), range(10, C - 1))):
                    put(6 + t, "dve", invert, f, cols)
            if early:
                put(6, "act", activate, a)
                put(7, "pe act dve", transpose_keys, a)
                put(8, "sp", store_keys, a)
                put(9, "sp", spread_keys, a, p)
            if front:
                put(10, "dve sp", store_inverse, f)
                put(10, "sp", load_inverse, f)
            if post:
                put(11, "pe", down, o_, 0, range(4))
            for slot in slots:
                for emit in slot:
                    emit()

        def program(e, eng):
            step(e, eng, -2, 0, chain=False, front=False, post=False, tail=False)
            step(e, eng, -1, 1, chain=False, post=False, tail=False)
            step(e, eng, 0, 0, post=False, tail=False)
            step(e, eng, 1, 1, tail=False)
            with eng.Fori(1, NS // 2 - 1) as i:
                step(e, eng, i * 2, 0)
                step(e, eng, i * 2 + 1, 1)
            step(e, eng, NS - 2, 0, early=False)
            step(e, eng, NS - 1, 1, front=False, early=False)
            step(e, eng, NS, 0, chain=False, front=False, early=False)
            step(e, eng, NS + 1, 1, chain=False, front=False, early=False, post=False)
            if e == "sp":
                done(eng, "out", NS - 1)

        as_u32 = lambda a: a.bitcast(mybir.dt.uint32)
        block = ctx.enter_context(nc.Block())
        w_nat = v[:, 0, 0:2, :]
        wg_nat = E[1][:, 0:4].rearrange("p h b i z n -> p (h b i z n)").bitcast(I32)[:, 0:NHT * D]\
            .rearrange("p (t d) -> p t d", t=NHT)
        wu_nat = E[1][:, 4:8].rearrange("p h b i z n -> p (h b i z n)").bitcast(I32)[:, 0:NHT * D]\
            .rearrange("p (t d) -> p t d", t=NHT)
        wd_nat = E[1][:, 8:12].rearrange("p h b i z n -> p (h b i z n)").bitcast(I32)[:, 0:2 * HID]\
            .rearrange("p (t d) -> p t d", t=2)
        wg16 = tb[:, 0:2].rearrange("p h b i z n -> p (h b i z n)")[:, 0:NHT * D]\
            .rearrange("p (t d) -> p t d", t=NHT)
        wu16 = tb[:, 2:4].rearrange("p h b i z n -> p (h b i z n)")[:, 0:NHT * D]\
            .rearrange("p (t d) -> p t d", t=NHT)
        wd16 = tb[:, 4:6].rearrange("p h b i z n -> p (h b i z n)")[:, 0:2 * HID]\
            .rearrange("p (t d) -> p t d", t=2)
        ps16 = [pg[0][:, 0:256].bitcast(F16), pg[1][:, 0:256].bitcast(F16)]

        jobs = []
        for dst, src in ((wg_t, wg16), (wu_t, wu16)):
            for half in range(2):
                for t0 in range(0, NHT, 2):
                    jobs.append(([src[:, t0 + a, half * P:(half + 1) * P] for a in range(2)],
                                 dst[:, half, t0 * P:(t0 + 2) * P]))
        for t in range(NHT):
            jobs.append(([wd16[:, a, t * P:(t + 1) * P] for a in range(2)], wd_t[:, t, :]))
        NJ = len(jobs)
        N_SETUP = 4 + 1 + 8 + 2 * C + 7 + 1 + (C - 1)

        @block.sync
        def _(eng):
            bc = lambda a, n: a.rearrange("(o n) -> o n", o=1).to_broadcast([P, n])
            eng.dma_start(sc[:, ETA:ETA + 1], eta.to_broadcast([P, 1])).then_inc(s_ld, 16)
            eng.dma_start(sc[:, LOGIT:LOGIT + 1], lam_logit.to_broadcast([P, 1])).then_inc(s_ld, 16)
            eng.dma_start(w_nat, W.rearrange("(a p) d -> p a d", p=P)).then_inc(s_ld, 16)
            eng.dma_start(wg_nat, w_gate.rearrange("(t p) d -> p t d", p=P)).then_inc(s_ld, 16)
            eng.dma_start(wu_nat, w_up.rearrange("(t p) d -> p t d", p=P)).then_inc(s_ld, 16)
            eng.dma_start(wd_nat, w_down.rearrange("(t p) d -> p t d", p=P)).then_inc(s_ld, 16)
            eng.dma_start(gamma[:, :], bc(ln_gamma, D)).then_inc(s_ld, 16)
            eng.dma_start(lnb[:, :], bc(ln_beta, D)).then_inc(s_ld, 16)
            eng.wait_ge(s_wt, NJ + 1)
            eng.wait_ge(s_pool0, 12)
            program("sp", eng)

        @block.gpsimd
        def _(eng):
            n = [0]
            chained(eng, eng.memset(ident[:, :], 0.0), n, s_pool0)
            chained(eng, eng.affine_select(out=ident[:, :], in_=ident[:, :], compare_op=ALU.not_equal, fill=1.0,
                                           base=0, pattern=[[-1, P]], channel_multiplier=1), n, s_pool0)
            chained(eng, eng.memset(mhalf[:, :], -0.5), n, s_pool0)
            chained(eng, eng.memset(eps[:, :], LN_EPS), n, s_pool0)
            chained(eng, eng.memset(epsq[:, :], LN_EPS / 4), n, s_pool0)
            chained(eng, eng.memset(minus[:, :], -1.0), n, s_pool0)
            chained(eng, eng.memset(as_u32(E[0][:, :, :, :, :, :].rearrange("p h b i z n -> p (h b i z n)")), 0), n, s_pool0)
            chained(eng, eng.memset(as_u32(kb[0][:, :, :, :, :, :].rearrange("p b k z h m -> p (b k z h m)")), 0), n, s_pool0)
            chained(eng, eng.memset(as_u32(kb[1][:, :, :, :, :, :].rearrange("p b k z h m -> p (b k z h m)")), 0), n, s_pool0)
            chained(eng, eng.memset(S[:, :], 0.0), n, s_pool0)
            eng.wait_ge(s_wt, NJ + 1)
            chained(eng, eng.memset(as_u32(E[1][:, :, :, :, :, :].rearrange("p h b i z n -> p (h b i z n)")), 0), n, s_pool0)
            chained(eng, eng.memset(as_u32(tb[:, :, :, :, :, :].rearrange("p h b i z n -> p (h b i z n)")), 0), n, s_pool0)
            eng.wait_ge(s_c, N_SETUP)
            program("pool", eng)

        @block.scalar
        def _(eng):
            eng.wait_ge(s_ld, 16 * 8)
            eng.activation(sc[:, OML:OML + 1], sc[:, LOGIT:LOGIT + 1], ACT.Sigmoid, scale=-1.0).then_inc(s_a0, 1)
            program("act", eng)

        @block.vector
        def _(eng):
            n = [0]

            def link(ins):
                chained(eng, ins, n, s_c)

            eng.wait_ge(s_pool0, 2)
            link(eng.tensor_copy(ident16[:, :], ident[:, :]))
            eng.wait_ge(s_ld, 16 * 8)
            link(eng.tensor_copy(wg16, wg_nat))
            link(eng.tensor_copy(wu16, wu_nat))
            link(eng.tensor_copy(wd16, wd_nat))
            n_w = n[0]
            for j, (_, dst) in enumerate(jobs):
                eng.wait_ge(s_ps, j + 1)
                eng.tensor_copy(dst, ps16[j % 2][:, 0:2 * P]).then_inc(s_wt, 1)
            eng.wait_ge(s_ps, NJ + 1)
            w_ps = pu[0][:, :].rearrange("p (a d) -> p a d", a=2)
            link(eng.tensor_scalar(w_t[:, :, 0, :], w_ps, WS, None, ALU.mult))
            eng.scalar_tensor_tensor(w_t[:, :, 1, :], w_ps, WS, w_t[:, :, 0, :], ALU.mult, ALU.subtract)\
               .then_inc(s_wt, 1)
            eng.wait_ge(s_a0, 1)
            link(eng.tensor_scalar(sc[:, LAM:LAM + 1], sc[:, OML:OML + 1], -1.0, 1.0, ALU.mult, ALU.add))
            link(eng.tensor_tensor(sc[:, BETA:BETA + 1], sc[:, ETA:ETA + 1], sc[:, OML:OML + 1], ALU.mult))
            link(eng.tensor_scalar(sc[:, BETA:BETA + 1], sc[:, BETA:BETA + 1], 1.0 / DH, None, ALU.mult))
            link(eng.tensor_scalar(sc[:, NBETA:NBETA + 1], sc[:, BETA:BETA + 1], -1.0, None, ALU.mult))
            link(eng.tensor_scalar(sc[:, BETAS:BETAS + 1], sc[:, BETA:BETA + 1], 1.0 / (KS * RS), None, ALU.mult))
            link(eng.tensor_scalar(sc[:, BETAR:BETAR + 1], sc[:, BETA:BETA + 1], 0.5 / RS, None, ALU.mult))
            link(eng.memset(powers[:, 0:1], 1.0))
            link(eng.memset(S16[:, :, :], 0.0))
            for m in range(C):
                link(eng.tensor_scalar(powers[:, m + 1:m + 2], powers[:, m:m + 1], sc[:, LAM:LAM + 1], None,
                                       ALU.mult))
            for m in range(C):
                link(eng.tensor_copy(rpowers[:, m:m + 1], powers[:, C - 1 - m:C - m]))
            link(eng.tensor_reduce(step_of[:, :], ident[:, :].rearrange("p (b i) -> p i b", b=B), AX.X, ALU.add))
            link(eng.tensor_tensor(ctmp[:, 0, :], step_of[:, :], powers[:, 1:C + 1], ALU.mult))
            link(eng.tensor_tensor(ctmp[:, 1, :], step_of[:, :], rpowers[:, :], ALU.mult))
            link(eng.tensor_reduce(dcol[:, :], ctmp[:, 0, :], AX.X, ALU.add))
            link(eng.tensor_scalar(dcol[:, :], dcol[:, :], -1.0 / (KS * SS), None, ALU.mult))
            link(eng.tensor_reduce(kcol[:, :], ctmp[:, 1, :], AX.X, ALU.add))
            link(eng.tensor_scalar(kcol[:, :], kcol[:, :], KS, None, ALU.mult))
            link(eng.memset(nmask[:, :, :], 0.0))
            flat = nmask[:, :, :].rearrange("p i j -> p (i j)")
            for d in range(1, C):
                link(eng.tensor_scalar(flat[:, C * d:C * C:C + 1],
                                       powers[:, d:d + 1].to_broadcast([P, C - d]),
                                       sc[:, NBETA:NBETA + 1], None, ALU.mult))
            assert n[0] == N_SETUP
            program("dve", eng)

        @block.tensor
        def _(eng):
            eng.wait_ge(s_pool0, 2)
            eng.wait_ge(s_c, 4)
            for j, (srcs, _) in enumerate(jobs):
                if j >= 2:
                    eng.wait_ge(s_wt, j - 1)
                for a, src in enumerate(srcs):
                    last = eng.transpose(ps16[j % 2][:, a * P:(a + 1) * P], src, ident16[:, :])
                last.then_inc(s_ps, 1)
            for half in range(2):
                for a in range(2):
                    last = eng.transpose(pu[0][:, half * D + a * P:half * D + (a + 1) * P],
                                         w_nat[:, a, half * P:(half + 1) * P], ident[:, :])
            last.then_inc(s_ps, 1)
            eng.wait_ge(s_wt, NJ + 1)
            program("pe", eng)


_INS = ['L0_attn_x', 'L0_attn_W', 'L0_attn_ln_gamma', 'L0_attn_ln_beta', 'L0_attn_eta', 'L0_attn_lam_logit',
        'L0_ffn_w_gate', 'L0_ffn_w_up', 'L0_ffn_w_down']


def kernel(**inputs):
    import numpy as _np
    import concourse.bacc as _bacc
    from concourse.bass_utils import run_bass_kernel_spmd as _run

    nc = _bacc.Bacc("TRN2", target_bir_lowering=False, num_devices=1)
    arrays, args = {}, []
    for name in _INS:
        a = _np.ascontiguousarray(inputs[name])
        if a.ndim == 0:
            a = a.reshape(1)
        arrays[name] = a
        args.append(nc.dram_tensor(name, a.shape, mybir.dt.from_np(a.dtype), kind="ExternalInput").ap())
    args.append(nc.dram_tensor("y_out", (B, L, D), F32, kind="ExternalOutput").ap())
    build(nc, *args)
    r = _run(nc, [arrays], core_ids=[0])
    return r.results[0]["y_out"]
```
